# Optimizing a Trainium2 kernel written in Bass

```python
import numpy as np
import jax
import jax.numpy as jnp

def _softmax(x, axis=-1):
    return jax.nn.softmax(x, axis=axis)

def _gelu(x):
    return jax.nn.gelu(x, approximate=True)

def _silu(x):
    return jax.nn.silu(x)

def _sigmoid(x):
    return jax.nn.sigmoid(x)

def _layernorm(x, axis=-1, eps=1e-05):
    m = jnp.mean(x, axis=axis, keepdims=True)
    v = jnp.var(x, axis=axis, keepdims=True)
    return (x - m) / jnp.sqrt(v + eps)

def _scatter_add(tgt, idx, src, axis=0):
    return tgt.at[idx].add(src)

def _segment_sum(src, seg, n):
    return jax.ops.segment_sum(src, seg, n)
kernel_name = 'mk_adj_preln_d2_adj_r2_b1ede9'

def setup_inputs(seed: int=0):
    np.random.seed(seed)
    _w = jnp.asarray

    def _rec_inputs():
        import jax
        import jax.numpy as jnp
        _gk = jax.random.key(seed)
        x = -0.000929 + 1 * jax.random.normal(jax.random.fold_in(_gk, 1), (4096, 128), jnp.float32)
        _a = jax.random.bernoulli(jax.random.fold_in(_gk, 2), 0.00390625, (4096, 4096))
        adj = _a.astype(jnp.int32)
        return (x, adj)
    x, adj = _rec_inputs()

    def _L0_gnn_setup():
        import jax, jax.numpy as jnp
        import numpy as np
        from jax import lax
        N = 4096
        D = 128
        CHUNK = 128
        key = jax.random.key(seed)
        k1, k2 = jax.random.split(key)
        x = jax.random.normal(k1, (N, D), dtype=jnp.float32)
        adj = jax.random.randint(k2, (N, N), 0, 2, dtype=jnp.int32)
        return {'x': x, 'adj': adj}
    _L0_gnn_all = _L0_gnn_setup()
    _L0_gnn_in = {k: v for k, v in _L0_gnn_all.items() if k in ()}
    del _L0_gnn_all

    def _L1_gnn_setup():
        import jax, jax.numpy as jnp
        import numpy as np
        N = 4096
        IN_F = 128
        OUT_F = 128
        ALPHA = 0.2
        NEG_FILL = -9000000000000000.0
        key = jax.random.key(seed)
        k_adj, k_h, k_w, k_a = jax.random.split(key, 4)
        adj = jax.random.randint(k_adj, (N, N), 0, 2, dtype=jnp.int32)
        h = jax.random.normal(k_h, (N, IN_F), dtype=jnp.float32)
        W = jax.random.normal(k_w, (IN_F, OUT_F), dtype=jnp.float32) * (2.0 / (IN_F + OUT_F)) ** 0.5
        a = jax.random.normal(k_a, (2 * OUT_F, 1), dtype=jnp.float32) * (2.0 / (2 * OUT_F + 1)) ** 0.5
        return {'adj': adj, 'h': h, 'W': W, 'a': a}
    _L1_gnn_all = _L1_gnn_setup()
    _L1_gnn_in = {k: v for k, v in _L1_gnn_all.items() if k in ('W', 'a')}
    del _L1_gnn_all
    return {'x': x, 'adj': adj, 'L1_gnn_W': _L1_gnn_in['W'], 'L1_gnn_a': _L1_gnn_in['a']}

def reference(x, adj, L1_gnn_W, L1_gnn_a):
    import jax
    import jax.numpy as jnp

    def _L0_gnn_ref(x, adj):
        import jax, jax.numpy as jnp
        import numpy as np
        from jax import lax
        N = 4096
        D = 128
        CHUNK = 128
        n, d = x.shape
        neg = jnp.finfo(x.dtype).min
        adj_chunks = adj.reshape(n // CHUNK, CHUNK, n)

        def step(carry, a):
            mask = a != 0
            masked = jnp.where(mask[:, :, None], x[None, :, :], neg)
            m = jnp.max(masked, axis=1)
            has_nbr = jnp.any(mask, axis=1)
            out = jnp.where(has_nbr[:, None], m, jnp.zeros((), x.dtype))
            return (carry, out)
        _, out = lax.scan(step, None, adj_chunks)
        return out.reshape(n, d)

    def _L1_gnn_ref(adj, h, W, a):
        import jax, jax.numpy as jnp
        import numpy as np
        N = 4096
        IN_F = 128
        OUT_F = 128
        ALPHA = 0.2
        NEG_FILL = -9000000000000000.0
        Wh = h @ W
        Wh1 = Wh @ a[:OUT_F, :]
        Wh2 = Wh @ a[OUT_F:, :]
        e = jax.nn.leaky_relu(Wh1 + Wh2.T, ALPHA)
        attention = jnp.where(adj > 0, e, jnp.float32(NEG_FILL))
        attention = jax.nn.softmax(attention, axis=1)
        h_prime = attention @ Wh
        return jax.nn.elu(h_prime)
    h = jnp.maximum(_layernorm(x, axis=-1), 0.0)
    x = x + _L0_gnn_ref(h, adj)
    h = jnp.maximum(_layernorm(x, axis=-1), 0.0)
    x = x + _L1_gnn_ref(adj, h, L1_gnn_W, L1_gnn_a)
    return x

_drawn_inputs = setup_inputs


def setup_inputs(seed=0):
    import zlib

    import numpy as np

    out = dict(_drawn_inputs(seed))
    spreads = {}
    factors = {}
    for name, (base, spread) in spreads.items():
        noise = np.random.default_rng([zlib.crc32(name.encode()), seed]).standard_normal(out[name].shape)
        drawn = base * np.exp(spread * noise) if base else spread * noise
        out[name] = jnp.asarray(drawn.astype(out[name].dtype))
    for name, factor in factors.items():
        out[name] = (out[name] * factor).astype(out[name].dtype)
    return out
```

```python
from contextlib import ExitStack

import concourse.bass as bass
from concourse import mybir
from concourse.alu_op_type import AluOpType as ALU

F32 = mybir.dt.float32
I32 = mybir.dt.int32
U32 = mybir.dt.uint32
ACT = mybir.ActivationFunctionType
X = mybir.AxisListType.X

P = 128
SEG = 128
TOP = 8
SLOTS = 40
SURE = 8
EPS = 1e-5
ALPHA = 0.2
NEG_FILL = -9000000000000000.0


def gnn_layers(nc, x, adj, W, a, out):
    N, D = x.shape
    T = N // P
    NSEG = N // SEG
    CAND = NSEG * TOP
    ctx = ExitStack()
    with ctx:
        def sb(name, shape, dt=F32):
            return ctx.enter_context(nc.sbuf_tensor(name, shape, dt))

        def ps(name, shape, dt=F32):
            return ctx.enter_context(nc.psum_tensor(name, shape, dt))

        def sem(name):
            return ctx.enter_context(nc.semaphore(name))

        h_rows = nc.dram_tensor("h_rows", [N, D], F32, kind="Internal").ap()

        x_sb = sb("x_sb", [P, T, D])
        nbr_max = sb("nbr_max", [P, T, D])
        h_sb = sb("h_sb", [P, T, D])
        Wh = sb("Wh", [P, T, D])
        t_all = sb("t_all", [P, N])
        adj_t = sb("adj_t", [P, 2, N], I32)
        key = sb("key", [P, N])
        count_down = sb("count_down", [P, N])
        G = sb("G", [P, 2, SLOTS, D])
        G0 = G[:, 0, 0:T, :]
        G1 = G[:, 1, 0:T, :]
        h2T = key
        WhT = count_down
        cand = sb("cand", [P, CAND])
        nbrs = sb("nbrs", [P, SLOTS])
        idx = sb("idx", [P, 2, SLOTS], U32)
        junk = sb("junk", [P, SLOTS])
        degree = sb("degree", [P, 1])
        key_sum = sb("key_sum", [P, 1])
        list_sum = sb("list_sum", [P, 1])
        missed = sb("missed", [P, T])
        missed_row = sb("missed_row", [P, 1])
        n_slots = sb("n_slots", [1, 2], I32)
        landed = sb("landed", [1, 2])
        landed_i = sb("landed_i", [1, 2], I32)
        deg_max = sb("deg_max", [1, 1])
        any_missed = sb("any_missed", [1, 1], I32)
        stat = sb("stat", [P, T])
        mean = sb("mean", [P, T])
        rstd = sb("rstd", [P, T])
        ident = sb("ident", [P, P])
        ones = sb("ones", [P, P])
        W_sb = sb("W_sb", [D, D])
        a_sb = sb("a_sb", [D, 2])
        a2_all = sb("a2_all", [D, P])
        s_col = sb("s_col", [P, T])
        neg_max = sb("neg_max", [P, 2])
        den = sb("den", [P, 2])
        rden = sb("rden", [P, 2])
        hp = sb("hp", [P, D])
        hm = sb("hm", [P, D])
        he = sb("he", [P, D])
        res = sb("res", [P, 2, D])

        p_small = ps("p_small", [P, 512])
        p_T = [ps(f"p_T{i}", [P, 512]) for i in range(2)]
        p_W = [ps(f"p_W{i}", [P, 512]) for i in range(2)]
        p_acc = [ps(f"p_acc{i}", [P, 512]) for i in range(2)]

        x_in = sem("x_in")
        w_in = sem("w_in")
        consts = sem("consts")
        a2_ready = sem("a2_ready")
        var_ready = sem("var_ready")
        std_ready = sem("std_ready")
        h_ready = sem("h_ready")
        h_stored = sem("h_stored")
        adj_in = [sem(f"adj_in{b}") for b in range(2)]
        key_done = sem("key_done")
        deg_ready = sem("deg_ready")
        degT_ready = sem("degT_ready")
        lists_ready = sem("lists_ready")
        zeroed = sem("zeroed")
        turn = sem("turn")
        gathered = [sem(f"gathered{b}") for b in range(2)]
        reduced = sem("reduced")
        miss_ready = sem("miss_ready")
        miss_sum = sem("miss_sum")
        miss_known = sem("miss_known")
        back_adj = sem("back_adj")
        back_h = [sem(f"back_h{b}") for b in range(2)]
        back_used = sem("back_used")
        back_tile = sem("back_tile")
        layer1 = sem("layer1")
        h2_ready = sem("h2_ready")
        hT_ready = sem("hT_ready")
        hT_copied = sem("hT_copied")
        W_mm = sem("W_mm")
        W_copied = sem("W_copied")
        adj2_in = [sem(f"adj2_in{b}") for b in range(2)]
        adj2_used = sem("adj2_used")
        z_ready = sem("z_ready")
        e_ready = sem("e_ready")
        eT_ready = sem("eT_ready")
        eT_copied = sem("eT_copied")
        av_ready = sem("av_ready")
        hm_ready = sem("hm_ready")
        he_ready = sem("he_ready")
        res_ready = sem("res_ready")
        stored = [sem(f"stored{b}") for b in range(2)]
        block = ctx.enter_context(nc.Block())

        rows = lambda v: v.rearrange("(t p) d -> p t d", p=P)
        adj_tiles = adj.rearrange("(t p) j -> t p j", p=P)
        out_tiles = out.rearrange("(t p) d -> t p d", p=P)
        h_chunks = h_rows.rearrange("(c r) d -> c (r d)", r=T)
        CH = N // T

        @block.sync
        def _(sp):
            for q in range(4):
                sp.dma_start(x_sb[:, q * T // 4:(q + 1) * T // 4], rows(x)[:, q * T // 4:(q + 1) * T // 4]).then_inc(x_in, 16)
            sp.dma_start(W_sb[:], W).then_inc(w_in, 16)
            for k in range(2):
                sp.dma_start(a_sb[:, k:k + 1], a[k * D:(k + 1) * D, :]).then_inc(w_in, 16)
            for b in range(2):
                sp.dma_start(adj_t[:, b], adj_tiles[b]).then_inc(adj_in[b], 16)
            sp.wait_ge(h_ready, 1)
            sp.dma_start(rows(h_rows), h_sb[:]).then_inc(h_stored, 16)
            with sp.Fori(1, T // 2) as i:
                for b in range(2):
                    sp.wait_ge(key_done, 2 * i + b - 1)
                    sp.dma_start(adj_t[:, b], adj_tiles[2 * i + b]).then_inc(adj_in[b], 16)
            sp.wait_ge(miss_known, 1)
            with sp.If(sp.value_load(any_missed[0:1, 0:1], min_val=0, max_val=1)):
                with sp.Fori(0, T) as t:
                    sp.wait_ge(back_tile, t + 1)
                    sp.dma_start(adj_t[:, 0], adj_tiles[t]).then_inc(back_adj, 16)
                    with sp.Fori(0, CH // 2) as c:
                        for b in range(2):
                            sp.wait_ge(back_used, t * CH + 2 * c + b + 1)
                            sp.dma_start(G[:, b, 0:T, :].rearrange("p r d -> p (r d)"),
                                         h_chunks[2 * c + b].partition_broadcast(P)).then_inc(back_h[b], 16)
            sp.wait_ge(layer1, 1)
            for b in range(2):
                sp.dma_start(adj_t[:, b], adj_tiles[b]).then_inc(adj2_in[b], 16)
            with sp.Fori(1, T // 2) as i:
                for b in range(2):
                    sp.wait_ge(adj2_used, 2 * i + b - 1)
                    sp.dma_start(adj_t[:, b], adj_tiles[2 * i + b]).then_inc(adj2_in[b], 16)
                    sp.wait_ge(res_ready, 2 * i + b - 1)
                    sp.dma_start(out_tiles[2 * i + b - 2], res[:, b]).then_inc(stored[b], 16)
            for b in range(2):
                sp.wait_ge(res_ready, T - 1 + b)
                sp.dma_start(out_tiles[T - 2 + b], res[:, b]).then_inc(stored[b], 16)
            for b in range(2):
                sp.wait_ge(stored[b], 16 * (T // 2))

        @block.gpsimd
        def _(pool):
            pool.iota(count_down[:], [[-1, N]], base=N, channel_multiplier=0,
                      allow_small_or_imprecise_dtypes=True).then_inc(consts, 1)
            pool.memset(ones[:], 1.0).then_inc(consts, 1)
            pool.wait_ge(consts, 2)
            pool.affine_select(out=ident[:], in_=ones[:], compare_op=ALU.is_equal, fill=0.0,
                               base=0, pattern=[[-1, P]], channel_multiplier=1).then_inc(consts, 1)
            pool.wait_ge(h_stored, 16)

            def gather(b, k):
                pool.indirect_dma_start(
                    G[:, b, k, :], None, h_rows, bass.IndirectOffsetOnAxis(ap=idx[:, b, k:k + 1], axis=0),
                    bounds_check=N - 1, oob_is_err=False).then_inc(gathered[b], 16)

            def gather_while(b, k, n):
                with pool.If(n > k):
                    gather(b, k)
                    if k + 1 < SLOTS:
                        gather_while(b, k + 1, n)

            with pool.Fori(0, T // 2) as i:
                for b in range(2):
                    pool.wait_ge(lists_ready, 2 * i + b + 1)
                    pool.wait_ge(zeroed, 2 * i + b + 1)
                    pool.sem_inc(turn, 1)
                    n = pool.value_load(n_slots[0:1, b:b + 1], min_val=0, max_val=SLOTS)
                    for k in range(SURE):
                        gather(b, k)
                    gather_while(b, SURE, n)

        @block.scalar
        def _(act):
            act.wait_ge(var_ready, 1)
            act.activation(rstd[:], stat[:], ACT.Sqrt).then_inc(std_ready, 1)
            for b in range(2):
                act.memzero(G[:, b]).then_inc(zeroed, 1)
            with act.Fori(1, T // 2) as i:
                for b in range(2):
                    act.wait_ge(reduced, 2 * i + b - 1)
                    act.memzero(G[:, b]).then_inc(zeroed, 1)
            act.wait_ge(var_ready, 2)
            act.activation(rstd[:], stat[:], ACT.Sqrt).then_inc(std_ready, 1)
            for g in range(T // 4):
                act.wait_ge(hT_ready, g + 1)
                act.activation(h2T[:, g * 512:(g + 1) * 512], p_T[g % 2][:], ACT.Copy).then_inc(hT_copied, 1)
            for g in range(T // 4):
                act.wait_ge(W_mm, 3 * g + 1)
                act.activation(WhT[:, g * 512:(g + 1) * 512], p_W[0][:], ACT.Copy).then_inc(W_copied, 1)
                act.wait_ge(W_mm, 3 * g + 2)
                act.activation(Wh[:, 4 * g:4 * g + 4, :], p_W[1][:], ACT.Copy).then_inc(W_copied, 1)
                act.wait_ge(W_mm, 3 * g + 3)
                act.activation(t_all[:, g * 512:(g + 1) * 512], p_T[0][:], ACT.Copy).then_inc(W_copied, 1)
                act.activation(s_col[:, 4 * g:4 * g + 4], p_small[:, 8:12], ACT.Copy).then_inc(W_copied, 1)

            def attend(i, b):
                t = 2 * i + b
                act.wait_ge(z_ready, t + 1)
                act.activation(G0, G0, ACT.Exp, bias=neg_max[:, b:b + 1], accum_out=den[:, b:b + 1]).then_inc(e_ready, 1)
                for g in range(T // 4):
                    act.wait_ge(eT_ready, t * (T // 4) + g + 1)
                    act.activation(h_sb[:, 4 * g:4 * g + 4, :], p_T[g % 2][:], ACT.Copy).then_inc(eT_copied, 1)
                act.wait_ge(hm_ready, t + 1)
                act.activation(he[:], hm[:], ACT.Exp).then_inc(he_ready, 1)

            with act.Fori(0, T // 2) as i:
                for b in range(2):
                    attend(i, b)

        @block.tensor
        def _(pe):
            pe.wait_ge(consts, 3)
            with pe.Fori(0, T) as t:
                pe.wait_ge(deg_ready, t + 1)
                pe.matmul(p_small[0:1, 0:P], degree[:], ident[:], start=True, stop=True).then_inc(degT_ready, 1)
            pe.wait_ge(miss_ready, 1)
            pe.matmul(p_small[0:1, 0:1], missed_row[:], ones[:, 0:1], start=True, stop=True).then_inc(miss_sum, 1)
            pe.wait_ge(h2_ready, 1)
            pe.wait_ge(w_in, 48)
            pe.wait_ge(a2_ready, 1)
            for g in range(T // 4):
                if g >= 2:
                    pe.wait_ge(hT_copied, g - 1)
                for q in range(4):
                    last = pe.transpose(p_T[g % 2][:, q * P:(q + 1) * P], h_sb[:, 4 * g + q, :], ident[:])
                last.then_inc(hT_ready, 1)
            for g in range(T // 4):
                pe.wait_ge(hT_copied, g + 1)
                if g:
                    pe.wait_ge(W_copied, 4 * g)
                else:
                    pe.wait_ge(hT_copied, T // 4)
                pe.matmul(p_W[0][:], W_sb[:], h2T[:, g * 512:(g + 1) * 512], start=True, stop=True).then_inc(W_mm, 1)
                for q in range(4):
                    last = pe.matmul(p_W[1][:, q * P:(q + 1) * P], h2T[:, (4 * g + q) * P:(4 * g + q + 1) * P], W_sb[:],
                                     start=True, stop=True)
                last.then_inc(W_mm, 1)
                pe.wait_ge(W_copied, 4 * g + 1)
                pe.matmul(p_T[0][:], a2_all[:], WhT[:, g * 512:(g + 1) * 512], start=True, stop=True)
                for q in range(4):
                    last = pe.matmul(p_small[:, 8 + q:9 + q], WhT[:, (4 * g + q) * P:(4 * g + q + 1) * P], a_sb[:, 0:1],
                                     start=True, stop=True)
                last.then_inc(W_mm, 1)

            def attend(t, b, first):
                pe.wait_ge(e_ready, t + 1)
                for g in range(T // 4):
                    if first and g < 2:
                        pe.wait_ge(W_copied, T)
                    else:
                        pe.wait_ge(eT_copied, t * (T // 4) + g - 1)
                    for q in range(4):
                        last = pe.transpose(p_T[g % 2][:, q * P:(q + 1) * P], G0[:, 4 * g + q, :], ident[:])
                    last.then_inc(eT_ready, 1)
                if not first:
                    pe.wait_ge(hm_ready, t - 1 if b else t)
                for g in range(T // 4):
                    pe.wait_ge(eT_copied, t * (T // 4) + g + 1)
                    for q in range(4):
                        j = 4 * g + q
                        last = pe.matmul(p_acc[b][:, 0:D], h_sb[:, j, :], Wh[:, j, :], start=(j == 0), stop=(j == T - 1))
                last.then_inc(av_ready, 1)

            attend(0, 0, True)
            attend(1, 1, False)
            with pe.Fori(1, T // 2) as i:
                for b in range(2):
                    attend(2 * i + b, b, False)

        @block.vector
        def _(dve):
            def link(ins):
                dve.drain()

            def loop(lo, hi, body):
                with dve.Fori(lo, hi) as i:
                    body(i)

            V = nc.vector
            over_d = lambda v: v.unsqueeze(2).to_broadcast([P, T, D])

            def layer_norm_relu(n):
                link(V.tensor_reduce(mean[:], x_sb[:], axis=X, op=ALU.add))
                link(V.tensor_scalar(mean[:], mean[:], 1.0 / D, None, ALU.mult))
                link(V.tensor_tensor(h_sb[:], x_sb[:], over_d(mean[:]), ALU.subtract))
                link(V.tensor_tensor(nbr_max[:], h_sb[:], h_sb[:], ALU.mult))
                link(V.tensor_reduce(stat[:], nbr_max[:], axis=X, op=ALU.add))
                link(V.tensor_scalar(stat[:], stat[:], 1.0 / D, EPS, ALU.mult, ALU.add))
                dve.sem_inc(var_ready, 1)
                dve.wait_ge(std_ready, n)
                link(V.reciprocal(rstd[:], rstd[:]))
                return V.scalar_tensor_tensor(h_sb[:], h_sb[:], 0.0, over_d(rstd[:]), ALU.max, ALU.mult)

            V.memset(landed[:], 0.0)
            dve.wait_ge(w_in, 48)
            dve.wait_ge(consts, 2)
            V.tensor_scalar(a2_all[:], ones[:], a_sb[:, 1:2], None, ALU.mult).then_inc(a2_ready, 1)
            dve.wait_ge(x_in, 64)
            layer_norm_relu(1).then_inc(h_ready, 1)
            dve.wait_ge(consts, 3)

            def find(i, b, first):
                t = 2 * i + b
                dve.wait_ge(adj_in[b], 16 * (i + 1))
                V.scalar_tensor_tensor(key[:], adj_t[:, b], 0, count_down[:], ALU.not_equal, ALU.mult,
                                       accum_out=key_sum[:]).then_inc(key_done, 1)
                dve.drain()
                for s in range(NSEG):
                    last = V.max(cand[:, s * TOP:(s + 1) * TOP], key[:, s * SEG:(s + 1) * SEG])
                link(last)
                for r in range(SLOTS // TOP):
                    link(V.max(nbrs[:, r * TOP:(r + 1) * TOP], cand[:]))
                    if r < SLOTS // TOP - 1:
                        link(V.match_replace(cand[:], nbrs[:, r * TOP:(r + 1) * TOP], cand[:], 0.0))
                V.tensor_reduce(list_sum[:], nbrs[:], axis=X, op=ALU.add)
                V.tensor_scalar(junk[:], nbrs[:], 0.0, None, ALU.is_gt, ALU.add, accum_out=degree[:]).then_inc(deg_ready, 1)
                link(V.tensor_scalar(idx[:, b], nbrs[:], -1.0, float(N), ALU.mult, ALU.add))
                V.tensor_tensor(missed[:, bass.ds(t, 1)], key_sum[:], list_sum[:], ALU.subtract)
                dve.wait_ge(degT_ready, t + 1)
                link(V.tensor_reduce(deg_max[:], p_small[0:1, 0:P], axis=X, op=ALU.max))
                link(V.tensor_scalar(deg_max[:], deg_max[:], float(SURE), None, ALU.max))
                V.tensor_copy(n_slots[:, b:b + 1], deg_max[:])
                link(V.scalar_tensor_tensor(landed[:, b:b + 1], deg_max[:], 16.0, landed[:, b:b + 1], ALU.mult, ALU.add))
                V.tensor_copy(landed_i[:, b:b + 1], landed[:, b:b + 1]).then_inc(lists_ready, 1)
                dve.drain()

            def reduce(i, b):
                t = 2 * i + b
                n = dve.value_load(landed_i[0:1, b:b + 1], min_val=0, max_val=16 * SLOTS * T)
                dve.wait_ge(gathered[b], n)
                V.tensor_reduce(nbr_max[:, bass.ds(t, 1), :].rearrange("p t d -> p (t d)"),
                                G[:, b].rearrange("p k d -> p d k"), axis=X, op=ALU.max).then_inc(reduced, 1)

            def first_tiles():
                find(0, 0, True)
                find(0, 1, True)
                reduce(0, 0)

            def both(i):
                find(i, 0, False)
                reduce(i - 1, 1)
                find(i, 1, False)
                reduce(i, 0)

            first_tiles()
            loop(1, T // 2, both)
            reduce(T // 2 - 1, 1)
            dve.drain()

            link(V.tensor_reduce(missed_row[:], missed[:], axis=X, op=ALU.max))
            dve.sem_inc(miss_ready, 1)
            dve.wait_ge(miss_sum, 1)
            V.tensor_scalar(any_missed[:], p_small[0:1, 0:1], 0.5, None, ALU.is_gt).then_inc(miss_known, 1)
            dve.wait_ge(miss_known, 1)
            with dve.If(dve.value_load(any_missed[0:1, 0:1], min_val=0, max_val=1)):
                dve.sem_inc(back_tile, 1)
                dve.sem_inc(back_used, 2)
                with dve.Fori(0, T) as t:
                    acc = nbr_max[:, bass.ds(t, 1), :].rearrange("p t d -> p (t d)")
                    dve.wait_ge(back_adj, 16 * (t + 1))
                    V.tensor_scalar(key[:], adj_t[:, 0], 0, None, ALU.not_equal).then_inc(back_tile, 1)
                    V.tensor_scalar(acc, ones[:], 0.0, None, ALU.mult)
                    dve.drain()
                    with dve.Fori(0, CH // 2) as c:
                        for b in range(2):
                            dve.wait_ge(back_h[b], t * (16 * CH // 2) + 16 * c + 16)
                            for r in range(T):
                                j = (2 * c + b) * T + r
                                V.scalar_tensor_tensor(acc, G[:, b, r, :], key[:, bass.ds(j, 1)], acc, ALU.mult, ALU.max)
                                dve.drain()
                            dve.sem_inc(back_used, 1)

            link(V.tensor_tensor(x_sb[:], x_sb[:], nbr_max[:], ALU.add))
            dve.sem_inc(layer1, 1)
            layer_norm_relu(2).then_inc(h2_ready, 1)
            dve.wait_ge(W_copied, T)

            def attend(i, b, first):
                t = 2 * i + b
                dve.wait_ge(adj2_in[b], 16 * (i + 1))
                if not first:
                    dve.wait_ge(eT_ready, t * (T // 4))
                Z = G0.rearrange("p k d -> p (k d)")
                M = G1.rearrange("p k d -> p (k d)")
                link(V.tensor_scalar(Z, t_all[:], s_col[:, bass.ds(t, 1)], None, ALU.add))
                link(V.scalar_tensor_tensor(Z, Z, ALPHA, Z, ALU.mult, ALU.max))
                V.tensor_scalar(M, adj_t[:, b], 0, -2.0 * NEG_FILL, ALU.is_gt, ALU.mult).then_inc(adj2_used, 1)
                dve.drain()
                link(V.scalar_tensor_tensor(Z, M, NEG_FILL, Z, ALU.add, ALU.min))
                V.tensor_reduce(neg_max[:, b:b + 1], Z, axis=X, op=ALU.max, negate=True).then_inc(z_ready, 1)
                dve.wait_ge(av_ready, t + 1)
                link(V.reciprocal(rden[:, b:b + 1], den[:, b:b + 1]))
                link(V.tensor_scalar(hp[:], p_acc[b][:, 0:D], rden[:, b:b + 1], None, ALU.mult))
                link(V.tensor_scalar(hm[:], hp[:], 0.0, None, ALU.min))
                dve.sem_inc(hm_ready, 1)
                if not first:
                    dve.wait_ge(stored[b], 16 * i)
                link(V.scalar_tensor_tensor(hp[:], hp[:], 0.0, x_sb[:, bass.ds(t, 1), :].rearrange("p t d -> p (t d)"), ALU.max, ALU.add))
                dve.wait_ge(he_ready, t + 1)
                V.scalar_tensor_tensor(res[:, b], he[:], -1.0, hp[:], ALU.add, ALU.add).then_inc(res_ready, 1)

            def pair(i):
                attend(i, 0, False)
                attend(i, 1, False)

            attend(0, 0, True)
            dve.wait_ge(eT_ready, T // 4)
            attend(0, 1, True)
            loop(1, T // 2, pair)


_INS = ["x", "adj", "L1_gnn_W", "L1_gnn_a"]


def kernel(**inputs):
    import numpy as np
    import concourse.bacc as bacc
    from concourse import mybir as mb
    from concourse.bass_utils import run_bass_kernel_spmd as run

    nc = bacc.Bacc("TRN2", target_bir_lowering=False, num_devices=1)
    arrays, args = {}, []
    for name in _INS:
        arr = np.ascontiguousarray(inputs[name])
        arrays[f"in_{name}"] = arr
        args.append(nc.dram_tensor(f"in_{name}", arr.shape, mb.dt.from_np(arr.dtype), kind="ExternalInput").ap())
    shape = inputs["x"].shape
    out = nc.dram_tensor("out", shape, mb.dt.float32, kind="ExternalOutput").ap()
    gnn_layers(nc, *args, out)
    r = run(nc, [arrays], core_ids=[0])
    return r.results[0]["out"]
```

```python
from contextlib import ExitStack

import concourse.bass as bass
from concourse import mybir
from concourse.alu_op_type import AluOpType as ALU

F32 = mybir.dt.float32
BF16 = mybir.dt.bfloat16
FP8 = mybir.dt.float8e4
U8 = mybir.dt.uint8
I32 = mybir.dt.int32
U32 = mybir.dt.uint32
ACT = mybir.ActivationFunctionType
X = mybir.AxisListType.X

P = 128
TOP = 8
SLOTS = 40
SURE = 8
GR = 4
EPS = 1e-5
ALPHA = 0.2
REST = 1.0 - ALPHA
NEG_FILL = -9000000000000000.0
SLACK = 1.001
LEAST_DEN = 1e-18
MOST_DEN = 1e30


def gnn_layers(nc, x, adj, W, a, out):
    N, D = x.shape
    T = N // P
    NG = T // GR
    GP = GR * P
    CAND = T * TOP
    KC = 512 // P
    NK = T // KC
    TB = 1024 // P
    NT = T // TB
    D1 = D + 1
    XC = 4
    XT = T // XC
    AHEAD = GR * NG
    LUMP = (NG + 1) // 2

    ctx = ExitStack()
    with ctx:
        def sb(name, shape, dt=F32):
            return ctx.enter_context(nc.sbuf_tensor(name, shape, dt))

        def ps(name, shape, dt=F32):
            return ctx.enter_context(nc.psum_tensor(name, shape, dt))

        def sem(name):
            return ctx.enter_context(nc.semaphore(name))

        h_rows = nc.dram_tensor("h_rows", [N, D], F32, kind="Internal").ap()
        maskT_rows = nc.dram_tensor("maskT_rows", [T, P, T, P], U8, kind="Internal").ap()

        adj_t = sb("adj_t", [P, 2, N], I32)
        x_sb = sb("x_sb", [P, T, D])
        G = sb("G", [P, 2, SLOTS, D])
        attended = sb("attended", [P, T, D1])
        Whg = sb("Whg", [P, T, D1])
        r_all = sb("r_all", [P, N])
        blocks = sb("blocks", [P, GR * GP + 2 * LUMP * GR * GP // 4])
        masks = sb("masks", [P, N])
        weights = blocks[:, 0:GR * GP].rearrange("p (j i) -> p j i", j=GR)
        M = blocks[:, GR * GP:].bitcast(U8).rearrange("p (b n i q) -> p b n i q", b=2, n=LUMP, i=GR)
        h_sb = blocks[:, 0:N].rearrange("p (t d) -> p t d", t=T)
        sign = masks[:, 0:N // 2].bitcast(BF16)
        maskT = masks[:, N // 2:].bitcast(FP8).rearrange("p (b t i) -> p b t i", b=2, t=T)
        mask_bytes = masks[:, N // 2:].bitcast(U8).rearrange("p (b t i) -> p b t i", b=2, t=T)
        assert GR * GP * 4 + 2 * LUMP * GR * GP <= blocks[:].free_nbytes()

        cand = sb("cand", [P, CAND])
        nbrs = sb("nbrs", [P, SLOTS])
        idx = sb("idx", [P, 2, SLOTS], U32)
        junk = sb("junk", [P, SLOTS])
        degree = sb("degree", [P, 1])
        sign_sum = sb("sign_sum", [P, 2])
        lost = sb("lost", [P, 2, T])
        lost_row = sb("lost_row", [P, 2])
        n_slots = sb("n_slots", [1, 2], I32)
        landed_i = sb("landed_i", [1, 2], I32)
        deg_max = sb("deg_max", [1, 1])
        deg_junk = sb("deg_junk", [1, P])
        redo = sb("redo", [1, 1], I32)
        nbr_row = sb("nbr_row", [P, D])
        stats = sb("stats", [P, XT, 6])
        mv = sb("mv", [P, T, 2])
        rstd = sb("rstd", [P, T])
        shift = sb("shift", [P, T])
        h2 = sb("h2", [P, GR, D])
        h2T_g = sb("h2T_g", [P, GP])
        WhT_g = sb("WhT_g", [P, GP])
        lam = sb("lam", [P, T])
        g_col = sb("g_col", [P, T])
        ident = sb("ident", [P, P])
        ident_b = sb("ident_b", [P, P], BF16)
        down_b = sb("down_b", [P, P], BF16)
        seg_b = sb("seg_b", [P, T, P], BF16)
        ones = sb("ones", [P, P])
        W_sb = sb("W_sb", [D, D])
        WT_sb = sb("WT_sb", [D, D])
        a_sb = sb("a_sb", [D, 2])
        a1_all = sb("a1_all", [D, P])
        a2_all = sb("a2_all", [D, P])
        Wa = sb("Wa", [D, 2])
        bound = sb("bound", [P, 2])
        r_bias = sb("r_bias", [P, 1])
        g_bias = sb("g_bias", [P, 1])
        s_col = sb("s_col", [P, T])
        neg_max = sb("neg_max", [P, 2])
        den = sb("den", [P, 2])
        rden = sb("rden", [P, T])
        hp = sb("hp", [P, D])
        hm = sb("hm", [P, D])
        he = sb("he", [P, D])
        res = sb("res", [P, 2, D])
        G0 = G[:, 0, 0:T, :]
        G1 = G[:, 1, 0:T, :]
        key = masks[:]
        nbr_max = attended[:].rearrange("p t d -> p (t d)")[:, 0:N].rearrange("p (t d) -> p t d", t=T)
        Wh = Whg[:].rearrange("p t d -> p (t d)")[:, 0:N].rearrange("p (t d) -> p t d", t=T)
        h2T = key
        WhT = adj_t[:, 1].bitcast(F32)

        p_T = [ps(f"p_T{i}", [P, 1024], BF16) for i in range(2)]
        p_key = [ps(f"p_key{i}", [P, 512]) for i in range(2)]
        p_att = [ps(f"p_att{i}", [P, 512]) for i in range(2)]
        p_grp = ps("p_grp", [P, 512])
        p_small = ps("p_small", [P, 512])

        x_in = [sem(f"x_in{c}") for c in range(XC)]
        w_in = sem("w_in")
        consts = sem("consts")
        a_ready = sem("a_ready")
        WT_ready = sem("WT_ready")
        WT_copied = sem("WT_copied")
        Wa_ready = sem("Wa_ready")
        Wa_sq = sem("Wa_sq")
        norm_ready = sem("norm_ready")
        bound_ready = sem("bound_ready")
        bias_ready = sem("bias_ready")
        var_ready = sem("var_ready")
        std_ready = sem("std_ready")
        h_ready = sem("h_ready")
        h_stored = sem("h_stored")
        adj_in = [sem(f"adj_in{b}") for b in range(2)]
        sign_ready = sem("sign_ready")
        T_ready = sem("T_ready")
        T_copied = sem("T_copied")
        mask_stored = [sem(f"mask_stored{b}") for b in range(2)]
        key_ready = sem("key_ready")
        key_used = sem("key_used")
        passed = sem("passed")
        act_passed = sem("act_passed")
        pe_passed = sem("pe_passed")
        sp_passed = sem("sp_passed")
        deg_ready = sem("deg_ready")
        degT_ready = sem("degT_ready")
        lists_ready = sem("lists_ready")
        zeroed = sem("zeroed")
        turn = sem("turn")
        gathered = [sem(f"gathered{b}") for b in range(2)]
        reduced = sem("reduced")
        shift_ready = sem("shift_ready")
        h2_ready = sem("h2_ready")
        grp_mm = sem("grp_mm")
        grp_copied = sem("grp_copied")
        M_in = [sem(f"M_in{b}") for b in range(2)]
        w_ready = sem("w_ready")
        w_used = sem("w_used")
        att_added = sem("att_added")
        norm_done = sem("norm_done")
        elu_in = sem("elu_in")
        elu_exp = sem("elu_exp")
        out_ready = sem("out_ready")
        out_stored = [sem(f"out_stored{b}") for b in range(2)]
        lost_ready = sem("lost_ready")
        lost_sum = sem("lost_sum")
        redo_known = sem("redo_known")
        x_again = sem("x_again")
        back_adj = sem("back_adj")
        back_h = [sem(f"back_h{b}") for b in range(2)]
        back_used = sem("back_used")
        back_tile = sem("back_tile")
        var2_ready = sem("var2_ready")
        std2_ready = sem("std2_ready")
        h2_all = sem("h2_all")
        hT_ready = sem("hT_ready")
        hT_copied = sem("hT_copied")
        W_mm = sem("W_mm")
        W_copied = sem("W_copied")
        adj2_in = [sem(f"adj2_in{b}") for b in range(2)]
        adj2_used = sem("adj2_used")
        z_ready = sem("z_ready")
        e_ready = sem("e_ready")
        eT_ready = sem("eT_ready")
        eT_copied = sem("eT_copied")
        av_ready = sem("av_ready")
        hm_ready = sem("hm_ready")
        he_ready = sem("he_ready")
        res_ready = sem("res_ready")
        stored = [sem(f"stored{b}") for b in range(2)]
        block = ctx.enter_context(nc.Block())

        rows = lambda v: v.rearrange("(t p) d -> p t d", p=P)
        adj_tiles = adj.rearrange("(t p) j -> t p j", p=P)
        out_tiles = out.rearrange("(t p) d -> t p d", p=P)
        out_groups = out.rearrange("(g q p) d -> g p q d", q=GR, p=P)
        h_chunks = h_rows.rearrange("(c r) d -> c (r d)", r=T)
        CH = N // T

        def lump(g, q):
            if q == 0:
                return 0, (g + 1) // 2, g * g, (g * g + 1) // 2
            if q == 1:
                return (g + 1) // 2, g // 2 + 1, g * g + (g + 1) // 2, ((g + 1) * (g + 1) + 1) // 2
            if q == 2:
                return 0, g // 2, g * g + g + 1, (g * g + g) // 2
            return g // 2, (g + 1) // 2, g * g + g + 1 + g // 2, ((g + 1) * (g + 2)) // 2

        def due(g, q):
            if q == GR - 1:
                return g, 0
            return None if isinstance(g, int) and g == 0 else (g - 1, q + 1)

        def group_of(g, q, d):
            return (d, g) if q < 2 else (g, d)

        def part(eng, g, q, lo, hi, body):
            first, n, number, _ = lump(g, q)
            if isinstance(g, int):
                for k in range(lo, min(hi, n)):
                    body(first + k, number + k, k)
                return
            most = lump(NG - 2 if q == 0 else NG - 3, q)[1]
            if lo >= most:
                return
            if hi - lo == 1:
                with eng.If(n > lo):
                    body(first + lo, number + lo, lo)
            else:
                with eng.If(n > lo), eng.Fori(lo, n) as k:
                    body(first + k, number + k, k)

        def over_groups(eng, step):
            for q in range(GR):
                step(0, q)
            with eng.Fori(1, NG - 1) as g:
                for q in range(GR):
                    step(g, q)

        def in_range(t):
            return t if isinstance(t, int) else nc.s_assert_within(
                t, 0, T - 1, skip_runtime_bounds_check_because="inside unless_last for the last group")

        def unless_last(eng, g, body):
            if isinstance(g, int):
                body()
            else:
                with eng.If(g < NG - 2):
                    body()

        def elu_pos(b):
            return G[:, b, 0:GR, :]

        def elu_neg(b):
            return G[:, b, GR:2 * GR, :]

        def elu_e(b):
            return G[:, b, 2 * GR:3 * GR, :]

        def elu_out(b):
            return G[:, b, 3 * GR:4 * GR, :]

        @block.sync
        def _(sp):
            for c in range(XC):
                sp.dma_start(x_sb[:, c * XT:(c + 1) * XT], rows(x)[:, c * XT:(c + 1) * XT]).then_inc(x_in[c], 16)
                if c == 0:
                    sp.dma_start(W_sb[:], W).then_inc(w_in, 16)
                    for k in range(2):
                        sp.dma_start(a_sb[:, k:k + 1], a[k * D:(k + 1) * D, :]).then_inc(w_in, 16)
            for b in range(2):
                sp.dma_start(adj_t[:, b], adj_tiles[b]).then_inc(adj_in[b], 16)
            for c in range(XC):
                sp.wait_ge(h_ready, c + 1)
                sp.dma_start(rows(h_rows)[:, c * XT:(c + 1) * XT], h_sb[:, c * XT:(c + 1) * XT]).then_inc(h_stored, 16)

            def load_adj(t, q):
                sp.wait_ge(sign_ready, t + 1)
                sp.dma_start(adj_t[:, q % 2], adj_tiles[in_range(t + 2)]).then_inc(adj_in[q % 2], 16)

            def store_mask(t, q):
                sp.wait_ge(T_copied, NT * (t + 1))
                sp.sem_inc(sp_passed, 1)
                sp.dma_start(maskT_rows[t], mask_bytes[:, q % 2]).then_inc(mask_stored[q % 2], 16)

            def load_lump(g, q):
                if q == 0:
                    for k in range(2):
                        sp.wait_ge(mask_stored[k], 16 * (GR // 2) * (g + 1))
                if isinstance(g, int) and lump(g, q)[1] == 0:
                    return
                b = q % 2

                def one(d, n, k):
                    I, J = group_of(g, q, d)
                    sp.dma_start(M[:, b, k] if isinstance(k, int) else M[:, b, bass.ds(k, 1)].rearrange("p n i q -> p (n i) q"),
                                 maskT_rows.rearrange("(I i) p (J j) r -> I J p i (j r)", i=GR, j=GR)[I, J])\
                        .then_inc(M_in[b], 16)

                read = ((g * (2 * g - 1) + 1) // 2, g * g, g * g + (g + 1) // 2, g * g + g + 1)[q]
                sp.wait_ge(w_ready, AHEAD + GR * read)
                sp.sem_inc(sp_passed, 1)
                part(sp, g, q, 0, LUMP, one)

            def step(g, q):
                t = GR * (g + 1) + q
                if q < 2:
                    load_adj(t, q)
                else:
                    unless_last(sp, g, lambda: load_adj(t, q))
                if not (q < 2 and isinstance(g, int) and g == 0):
                    load_lump(*((g - 1, q + 2) if q < 2 else (g, q - 2)))
                store_mask(t, q)

            for q in range(GR):
                load_adj(q, q)
                store_mask(q, q)
            over_groups(sp, step)

            def store_out(g, b):
                sp.wait_ge(out_ready, g + 1)
                sp.dma_start(out_groups[g], elu_out(b)).then_inc(out_stored[b], 16)
            load_lump(NG - 2, 2)
            load_lump(NG - 2, 3)
            for q, groups in enumerate(((), (0, 1), (2, 3, 4), (5, 6, 7))):
                load_lump(NG - 1, q)
                for g in groups:
                    store_out(g, g % 2)
            for b in range(2):
                sp.wait_ge(out_stored[b], 16 * NG // 2)

            sp.wait_ge(redo_known, 1)
            with sp.If(sp.value_load(redo[0:1, 0:1], min_val=0, max_val=1)):
                for c in range(XC):
                    sp.dma_start(x_sb[:, c * XT:(c + 1) * XT], rows(x)[:, c * XT:(c + 1) * XT]).then_inc(x_again, 16)
                with sp.Fori(0, T) as t:
                    sp.wait_ge(back_tile, t + 1)
                    sp.dma_start(adj_t[:, 0], adj_tiles[t]).then_inc(back_adj, 16)
                    with sp.Fori(0, CH // 2) as c:
                        for b in range(2):
                            sp.wait_ge(back_used, t * CH + 2 * c + b + 1)
                            sp.dma_start(G[:, b, 0:T, :].rearrange("p r d -> p (r d)"),
                                         h_chunks[2 * c + b].partition_broadcast(P)).then_inc(back_h[b], 16)
                sp.wait_ge(W_copied, T)
                for b in range(2):
                    sp.dma_start(adj_t[:, b], adj_tiles[b]).then_inc(adj2_in[b], 16)
                with sp.Fori(1, T // 2) as i:
                    for b in range(2):
                        sp.wait_ge(adj2_used, 2 * i + b - 1)
                        sp.dma_start(adj_t[:, b], adj_tiles[2 * i + b]).then_inc(adj2_in[b], 16)
                        sp.wait_ge(res_ready, 2 * i + b - 1)
                        sp.dma_start(out_tiles[2 * i + b - 2], res[:, b]).then_inc(stored[b], 16)
                for b in range(2):
                    sp.wait_ge(res_ready, T - 1 + b)
                    sp.dma_start(out_tiles[T - 2 + b], res[:, b]).then_inc(stored[b], 16)
                for b in range(2):
                    sp.wait_ge(stored[b], 16 * (T // 2))

        @block.gpsimd
        def _(pool):
            pool.memset(ones[:], 1.0).then_inc(consts, 1)
            pool.iota(seg_b[:], [[-P, T], [0, P]], base=N - P, channel_multiplier=0,
                      allow_small_or_imprecise_dtypes=True).then_inc(consts, 1)
            pool.iota(down_b[:], [[0, P]], base=P, channel_multiplier=-1,
                      allow_small_or_imprecise_dtypes=True).then_inc(consts, 1)
            pool.wait_ge(consts, 3)
            for m, src in ((ident, ones), (ident_b, ones), (down_b, down_b)):
                pool.affine_select(out=m[:], in_=src[:], compare_op=ALU.is_equal, fill=0.0,
                                   base=0, pattern=[[-1, P]], channel_multiplier=1).then_inc(consts, 1)
            pool.affine_select(out=seg_b[:], in_=seg_b[:], compare_op=ALU.is_equal, fill=0.0,
                               base=0, pattern=[[0, T], [-1, P]], channel_multiplier=1).then_inc(consts, 1)
            pool.wait_ge(h_stored, 16 * XC)

            def gather(b, k):
                pool.indirect_dma_start(
                    G[:, b, k, :], None, h_rows, bass.IndirectOffsetOnAxis(ap=idx[:, b, k:k + 1], axis=0),
                    bounds_check=N - 1, oob_is_err=False).then_inc(gathered[b], 16)

            def gather_while(b, k, n):
                with pool.If(n > k):
                    gather(b, k)
                    if k + 1 < SLOTS:
                        gather_while(b, k + 1, n)

            with pool.Fori(0, T // 2) as i:
                for b in range(2):
                    pool.wait_ge(lists_ready, 2 * i + b + 1)
                    pool.wait_ge(zeroed, 2 * i + b + 1)
                    pool.sem_inc(turn, 1)
                    n = pool.value_load(n_slots[0:1, b:b + 1], min_val=0, max_val=SLOTS)
                    for k in range(SURE):
                        gather(b, k)
                    gather_while(b, SURE, n)

        @block.scalar
        def _(act):
            act.wait_ge(WT_ready, 1)
            act.activation(WT_sb[:], p_grp[:, 0:D], ACT.Copy).then_inc(WT_copied, 1)
            act.wait_ge(norm_ready, 1)
            act.activation(bound[:], p_small[:, 0:2], ACT.Sqrt, scale=float(D)).then_inc(bound_ready, 1)
            for c in range(XC):
                tiles = slice(c * XT, (c + 1) * XT)
                act.wait_ge(var_ready, c + 1)
                act.activation(rstd[:, tiles], rstd[:, tiles], ACT.Sqrt).then_inc(std_ready, 1)
                act.wait_ge(shift_ready, c + 1)
                for t in range(c * XT, (c + 1) * XT):
                    last = act.activation(h_sb[:, t, :], x_sb[:, t, :], ACT.Relu, bias=shift[:, t:t + 1], scale=rstd[:, t:t + 1])
                last.then_inc(h_ready, 1)

            def wait(s, value):
                act.wait_ge(s, value)
                act.sem_inc(act_passed, 1)

            def mask(t, b, turn2):
                act.wait_ge(adj_in[b], 16 * (turn2 + 1))
                if not (isinstance(t, int) and t == 0):
                    act.wait_ge(T_ready, NT * t)
                act.activation(sign, adj_t[:, b], ACT.Sign, accum_out=sign_sum[:, b:b + 1]).then_inc(sign_ready, 1)
                if not (isinstance(t, int) and t < 2):
                    act.wait_ge(mask_stored[b], 16 * turn2)
                    act.wait_ge(key_ready, NK * (t - 1))
                for k in range(NT):
                    wait(T_ready, NT * t + k + 1)
                    act.activation(maskT[:, b, k * TB:(k + 1) * TB, :], p_T[k % 2][:], ACT.Relu, saturate=False).then_inc(T_copied, 1)

            def zero(t, b):
                if not (isinstance(t, int) and t < 2):
                    act.wait_ge(reduced, t - 1)
                act.memzero(G[:, b]).then_inc(zeroed, 1)

            def norm(g):
                act.wait_ge(var_ready, XC + g + 1)
                act.activation(rstd[:, 0:GR], rstd[:, 0:GR], ACT.Sqrt).then_inc(std_ready, 1)
                act.wait_ge(shift_ready, XC + g + 1)
                for q in range(GR):
                    last = act.activation(h2[:, q, :], x_sb[:, bass.ds(GR * g + q, 1), :].rearrange("p t d -> p (t d)"),
                                          ACT.Relu, bias=shift[:, q:q + 1], scale=rstd[:, q:q + 1])
                last.then_inc(h2_ready, 1)

            def group(g):
                tiles = bass.ds(GR * g, GR)
                act.wait_ge(grp_mm, 4 * g + 1)
                act.activation(h2T_g[:], p_grp[:], ACT.Copy).then_inc(grp_copied, 1)
                act.wait_ge(grp_mm, 4 * g + 2)
                act.activation(WhT_g[:], p_grp[:], ACT.Copy).then_inc(grp_copied, 1)
                act.wait_ge(grp_mm, 4 * g + 3)
                act.activation(r_all[:, bass.ds(GP * g, GP)], p_grp[:], ACT.Exp, bias=r_bias[:], scale=REST)
                act.activation(lam[:, tiles], p_small[:, P:P + GR], ACT.Exp, bias=r_bias[:], scale=-REST)
                act.activation(g_col[:, tiles], p_small[:, P:P + GR], ACT.Exp, bias=g_bias[:]).then_inc(grp_copied, 1)
                wait(grp_mm, 4 * g + 4)
                act.drain()
                for q in range(GR):
                    t = bass.ds(GR * g + q, 1)
                    act.activation(Whg[:, t, 0:D].rearrange("p t d -> p (t d)"), p_grp[:, q * P:(q + 1) * P], ACT.Copy,
                                   scale=g_col[:, t])
                act.activation(Whg[:, tiles, D:D1].rearrange("p t o -> p (t o)"), g_col[:, tiles], ACT.Copy).then_inc(grp_copied, 1)

            mask(0, 0, 0)
            act.memzero(attended[:]).then_inc(norm_done, 1)
            zero(0, 0)
            mask(1, 1, 0)
            zero(1, 1)
            act.wait_ge(bias_ready, 1)
            act.wait_ge(lists_ready, 1)
            for q in range(2, GR):
                mask(q, q % 2, q // 2)
                zero(q, q % 2)

            def step(g, q):
                t = GR * (g + 1) + q
                mask(t, q % 2, 2 * (g + 1) + q // 2)
                zero(t, q % 2)
                if q == 1:
                    norm(g)
                if q == 2:
                    group(g)

            over_groups(act, step)
            norm(NG - 1)
            group(NG - 1)
            for g in range(NG):
                act.wait_ge(elu_in, g + 1)
                act.activation(elu_e(g % 2), elu_neg(g % 2), ACT.Exp).then_inc(elu_exp, 1)

            act.wait_ge(redo_known, 1)
            with act.If(act.value_load(redo[0:1, 0:1], min_val=0, max_val=1)):
                act.wait_ge(var2_ready, 1)
                act.activation(rstd[:], rstd[:], ACT.Sqrt).then_inc(std2_ready, 1)
                for g in range(T // 4):
                    act.wait_ge(hT_ready, g + 1)
                    act.activation(h2T[:, g * 512:(g + 1) * 512], p_key[g % 2][:], ACT.Copy).then_inc(hT_copied, 1)
                for g in range(T // 4):
                    act.wait_ge(W_mm, 3 * g + 1)
                    act.activation(WhT[:, g * 512:(g + 1) * 512], p_att[0][:], ACT.Copy).then_inc(W_copied, 1)
                    act.wait_ge(W_mm, 3 * g + 2)
                    act.activation(Wh[:, 4 * g:4 * g + 4, :], p_att[1][:], ACT.Copy).then_inc(W_copied, 1)
                    act.wait_ge(W_mm, 3 * g + 3)
                    act.activation(r_all[:, g * 512:(g + 1) * 512], p_key[0][:], ACT.Copy).then_inc(W_copied, 1)
                    act.activation(s_col[:, 4 * g:4 * g + 4], p_small[:, 8:12], ACT.Copy).then_inc(W_copied, 1)
                with act.Fori(0, T // 2) as i:
                    for b in range(2):
                        t = 2 * i + b
                        act.wait_ge(z_ready, t + 1)
                        act.activation(G0, G0, ACT.Exp, bias=neg_max[:, b:b + 1], accum_out=den[:, b:b + 1]).then_inc(e_ready, 1)
                        for g in range(T // 4):
                            act.wait_ge(eT_ready, t * (T // 4) + g + 1)
                            act.activation(h_sb[:, 4 * g:4 * g + 4, :], p_key[g % 2][:], ACT.Copy).then_inc(eT_copied, 1)
                        act.wait_ge(hm_ready, t + 1)
                        act.activation(he[:], hm[:], ACT.Exp).then_inc(he_ready, 1)

        @block.tensor
        def _(pe):
            pe.wait_ge(consts, 7)
            pe.wait_ge(w_in, 48)
            pe.transpose(p_grp[:, 0:D], W_sb[:], ident[:]).then_inc(WT_ready, 1)
            pe.wait_ge(WT_copied, 1)
            pe.matmul(p_small[:, 0:2], WT_sb[:], a_sb[:], start=True, stop=True).then_inc(Wa_ready, 1)
            pe.wait_ge(Wa_sq, 1)
            pe.matmul(p_small[:, 0:2], ones[:], Wa[:], start=True, stop=True).then_inc(norm_ready, 1)
            pe.wait_ge(bound_ready, 1)

            def transposes(t):
                pe.wait_ge(sign_ready, t + 1)
                for k in range(NT):
                    if not (isinstance(t, int) and NT * t + k < 2):
                        pe.wait_ge(T_copied, NT * t + k - 1)
                    for s in range(TB):
                        j = k * TB + s
                        last = pe.transpose(p_T[k % 2][:, s * P:(s + 1) * P], sign[:, j * P:(j + 1) * P], ident_b[:])
                    last.then_inc(T_ready, 1)

            def keys(t, b):
                for c in range(NK):
                    pe.wait_ge(T_copied, NT * t + c * KC // TB + 1)
                    if not (isinstance(t, int) and NK * t + c < 2):
                        pe.wait_ge(key_used, NK * t + c - 1)
                    pe.sem_inc(pe_passed, 1)
                    for s in range(KC):
                        one, seg = maskT[:, b, c * KC + s, :], p_key[c % 2][:, s * P:(s + 1) * P]
                        pe.matmul(seg, one, down_b[:], start=True, stop=False)
                        last = pe.matmul(seg, one, seg_b[:, c * KC + s, :], start=False, stop=True)
                    last.then_inc(key_ready, 1)

            def turn_degree(t):
                pe.wait_ge(deg_ready, t + 1)
                pe.matmul(p_small[0:1, 0:P], degree[:], ident[:], start=True, stop=True).then_inc(degT_ready, 1)

            def group(g):
                pe.wait_ge(h2_ready, g + 1)
                if not (isinstance(g, int) and g == 0):
                    pe.wait_ge(grp_copied, 4 * g)
                pe.wait_ge(lists_ready, GR * (g + 1) + (GR - 1 if isinstance(g, int) and g < NG - 1 or not isinstance(g, int) else 0))
                for q in range(GR):
                    last = pe.transpose(p_grp[:, q * P:(q + 1) * P], h2[:, q, :], ident[:])
                last.then_inc(grp_mm, 1)
                pe.wait_ge(grp_copied, 4 * g + 1)
                pe.matmul(p_grp[:], W_sb[:], h2T_g[:], start=True, stop=True).then_inc(grp_mm, 1)
                pe.wait_ge(grp_copied, 4 * g + 2)
                for q in range(GR):
                    pe.matmul(p_small[:, P + q:P + q + 1], WhT_g[:, q * P:(q + 1) * P], a_sb[:, 1:2], start=True, stop=True)
                pe.matmul(p_grp[:], a1_all[:], WhT_g[:], start=True, stop=True).then_inc(grp_mm, 1)
                pe.wait_ge(grp_copied, 4 * g + 3)
                for q in range(GR):
                    last = pe.matmul(p_grp[:, q * P:(q + 1) * P], h2T_g[:, q * P:(q + 1) * P], W_sb[:], start=True, stop=True)
                last.then_inc(grp_mm, 1)

            def attend(g, q, lo=0, hi=LUMP):
                def one(d, n, k):
                    I, J = group_of(g, q, d)
                    pe.wait_ge(att_added, n + 1)
                    for j in range(GR):
                        pe.wait_ge(w_ready, AHEAD + GR * n + j + 1)
                        for i in range(GR):
                            last = pe.matmul(p_att[i // 2][:, i % 2 * D1:(i % 2 + 1) * D1], weights[:, j, i * P:(i + 1) * P],
                                             Whg[:, bass.ds(GR * J + j, 1), :].rearrange("p t d -> p (t d)"),
                                             start=(j == 0 and i % 2 == 0), stop=(j == GR - 1 and i % 2 == 1),
                                             skip_group_check=True)
                        last.then_inc(w_used, 1)
                if lo == 0:
                    pe.wait_ge(grp_copied, 4 * g + 4)
                part(pe, g, q, lo, hi, one)

            transposes(0)
            for q in range(GR):
                keys(q, q % 2)
                transposes(q + 1)
                turn_degree(q)

            def step(g, q):
                t = GR * (g + 1) + q
                now = due(g, q)
                keys(t, q % 2)
                if q < 2:
                    transposes(t + 1)
                elif q == 3:
                    unless_last(pe, g, lambda: transposes(t + 1))
                if now:
                    attend(*now, 0, 1)
                turn_degree(t)
                if now:
                    attend(*now, 1, 2)
                    attend(*now, 2, LUMP)
                if q == 2:
                    group(g)
                    transposes(t + 1)

            over_groups(pe, step)
            for q in range(1, GR):
                attend(NG - 2, q)
            group(NG - 1)
            for q in range(GR):
                attend(NG - 1, q)
            pe.wait_ge(lost_ready, 1)
            pe.matmul(p_small[0:1, 0:1], lost_row[:, 0:1], ones[:, 0:1], start=True, stop=True).then_inc(lost_sum, 1)

            pe.wait_ge(redo_known, 1)
            with pe.If(pe.value_load(redo[0:1, 0:1], min_val=0, max_val=1)):
                pe.wait_ge(h2_all, 1)
                for g in range(T // 4):
                    if g >= 2:
                        pe.wait_ge(hT_copied, g - 1)
                    for q in range(4):
                        last = pe.transpose(p_key[g % 2][:, q * P:(q + 1) * P], h_sb[:, 4 * g + q, :], ident[:])
                    last.then_inc(hT_ready, 1)
                for g in range(T // 4):
                    pe.wait_ge(hT_copied, g + 1)
                    if g:
                        pe.wait_ge(W_copied, 4 * g)
                    else:
                        pe.wait_ge(hT_copied, T // 4)
                    pe.matmul(p_att[0][:], W_sb[:], h2T[:, g * 512:(g + 1) * 512], start=True, stop=True).then_inc(W_mm, 1)
                    for q in range(4):
                        last = pe.matmul(p_att[1][:, q * P:(q + 1) * P], h2T[:, (4 * g + q) * P:(4 * g + q + 1) * P], W_sb[:],
                                         start=True, stop=True)
                    last.then_inc(W_mm, 1)
                    pe.wait_ge(W_copied, 4 * g + 1)
                    pe.matmul(p_key[0][:], a2_all[:], WhT[:, g * 512:(g + 1) * 512], start=True, stop=True)
                    for q in range(4):
                        last = pe.matmul(p_small[:, 8 + q:9 + q], WhT[:, (4 * g + q) * P:(4 * g + q + 1) * P], a_sb[:, 0:1],
                                         start=True, stop=True)
                    last.then_inc(W_mm, 1)

                def attend_row(t, b, first):
                    pe.wait_ge(e_ready, t + 1)
                    for g in range(T // 4):
                        if first and g < 2:
                            pe.wait_ge(W_copied, T)
                        else:
                            pe.wait_ge(eT_copied, t * (T // 4) + g - 1)
                        for q in range(4):
                            last = pe.transpose(p_key[g % 2][:, q * P:(q + 1) * P], G0[:, 4 * g + q, :], ident[:])
                        last.then_inc(eT_ready, 1)
                    if not first:
                        pe.wait_ge(hm_ready, t - 1 if b else t)
                    for g in range(T // 4):
                        pe.wait_ge(eT_copied, t * (T // 4) + g + 1)
                        for q in range(4):
                            j = 4 * g + q
                            last = pe.matmul(p_att[b][:, 0:D], h_sb[:, j, :], Wh[:, j, :], start=(j == 0), stop=(j == T - 1))
                    last.then_inc(av_ready, 1)

                attend_row(0, 0, True)
                attend_row(1, 1, False)
                with pe.Fori(1, T // 2) as i:
                    for b in range(2):
                        attend_row(2 * i + b, b, False)

        @block.vector
        def _(dve):
            V = nc.vector

            def then(ins):
                dve.drain()
                return ins

            def wait(s, value):
                dve.wait_ge(s, value)
                dve.sem_inc(passed, 1)

            then(V.memset(landed_i[:], 0))
            dve.sem_inc(w_used, GR)
            dve.sem_inc(w_ready, AHEAD)
            dve.sem_inc(att_added, 1)
            dve.wait_ge(w_in, 48)
            dve.wait_ge(consts, 1)
            V.tensor_scalar(a1_all[:], ones[:], a_sb[:, 0:1], None, ALU.mult)
            V.tensor_scalar(a2_all[:], ones[:], a_sb[:, 1:2], None, ALU.mult).then_inc(a_ready, 1)
            dve.wait_ge(Wa_ready, 1)
            then(V.tensor_copy(bound[:], p_small[:, 0:2]))
            V.tensor_tensor(Wa[:], bound[:], bound[:], ALU.mult).then_inc(Wa_sq, 1)
            dve.wait_ge(bound_ready, 1)
            then(V.tensor_scalar(g_bias[:], bound[:, 1:2], -SLACK, None, ALU.mult))
            then(V.tensor_tensor(r_bias[:], bound[:, 0:1], bound[:, 1:2], ALU.max))
            V.tensor_scalar(r_bias[:], r_bias[:], -REST * SLACK, None, ALU.mult).then_inc(bias_ready, 1)

            def moments(t, q):
                tile = x_sb[:, bass.ds(t, 1), :].rearrange("p t d -> p (t d)")
                then(V.bn_stats(stats[:, 0, :], tile))
                V.bn_aggr(mv[:, q, :], stats[:, 0, :])

            def variance(tiles):
                dve.drain()
                return V.tensor_scalar(rstd[:, tiles], mv[:, tiles, 1:2].rearrange("p t o -> p (t o)"), EPS, None, ALU.add)

            def scale_and_shift(tiles):
                then(V.reciprocal(rstd[:, tiles], rstd[:, tiles]))
                return V.scalar_tensor_tensor(shift[:, tiles], mv[:, tiles, 0:1].rearrange("p t o -> p (t o)"), -1.0,
                                              rstd[:, tiles], ALU.mult, ALU.mult)

            for c in range(XC):
                dve.wait_ge(x_in[c], 16)
                for t in range(XT):
                    V.bn_stats(stats[:, t, :], x_sb[:, c * XT + t, :])
                dve.drain()
                for t in range(XT):
                    V.bn_aggr(mv[:, c * XT + t, :], stats[:, t, :])
                variance(slice(c * XT, (c + 1) * XT)).then_inc(var_ready, 1)
                dve.wait_ge(std_ready, c + 1)
                scale_and_shift(slice(c * XT, (c + 1) * XT)).then_inc(shift_ready, 1)
            dve.wait_ge(h_ready, XC)

            def find(t, b):
                for c in range(NK):
                    wait(key_ready, NK * t + c + 1)
                    for s in range(KC):
                        j = c * KC + s
                        last = V.max(cand[:, j * TOP:(j + 1) * TOP], p_key[c % 2][:, s * P:(s + 1) * P])
                    last.then_inc(key_used, 1)

            def lists(t, b):
                dve.drain()
                V.tensor_reduce(lost[:, 0, bass.ds(t, 1)], cand[:].rearrange("p (s k) -> p s k", k=TOP)[:, :, TOP - 1], axis=X, op=ALU.max)
                for r in range(SLOTS // TOP):
                    then(V.max(nbrs[:, r * TOP:(r + 1) * TOP], cand[:]))
                    if r < SLOTS // TOP - 1:
                        then(V.match_replace(cand[:], nbrs[:, r * TOP:(r + 1) * TOP], cand[:], 0.0))
                V.tensor_scalar(junk[:], nbrs[:], 0.0, None, ALU.is_gt, ALU.add, accum_out=degree[:]).then_inc(deg_ready, 1)
                V.tensor_scalar(idx[:, b], nbrs[:], -1.0, float(N), ALU.mult, ALU.add)
                dve.drain()
                V.scalar_tensor_tensor(lost[:, 1, bass.ds(t, 1)], sign_sum[:, b:b + 1], degree[:], nbrs[:, SLOTS - 1:SLOTS],
                                       ALU.not_equal, ALU.max)
                dve.wait_ge(degT_ready, t + 1)
                then(V.tensor_scalar(deg_junk[:], p_small[0:1, 0:P], float(SURE), None, ALU.max, ALU.max, accum_out=deg_max[:]))
                V.tensor_copy(n_slots[:, b:b + 1], deg_max[:])
                V.scalar_tensor_tensor(landed_i[:, b:b + 1], deg_max[:], 16.0, landed_i[:, b:b + 1], ALU.mult, ALU.add)
                dve.drain()
                dve.sem_inc(lists_ready, 1)

            def reduce(t, b):
                tile = x_sb[:, bass.ds(t, 1), :].rearrange("p t d -> p (t d)")
                n = dve.value_load(landed_i[0:1, b:b + 1], min_val=16, max_val=16 * SLOTS * T)
                dve.wait_ge(gathered[b], n)
                then(V.tensor_reduce(nbr_row[:], G[:, b].rearrange("p k d -> p d k"), axis=X, op=ALU.max).then_inc(reduced, 1))
                V.tensor_tensor(tile, tile, nbr_row[:], ALU.add)

            def attend_in(g, q):
                wait(grp_copied, 4 * g + 4)
                wait(M_in[q % 2], 16 * lump(g, q)[3])

            def weigh(g, q, d, n, k):
                I, J = group_of(g, q, d)
                r = r_all[:, bass.ds(GP * I, GP)].rearrange("p (i r) -> p i r", i=GR)
                for j in range(GR):
                    dve.wait_ge(w_used, GR * n + j + 1)
                    mask = (M[:, q % 2, k, :, j * P:(j + 1) * P] if isinstance(k, int) else
                            M[:, q % 2, bass.ds(k, 1), :, j * P:(j + 1) * P].rearrange("p n i q -> p (n i) q"))
                    V.scalar_tensor_tensor(weights[:, j, :].rearrange("p (i r) -> p i r", i=GR), r,
                                           lam[:, bass.ds(GR * J + j, 1)], mask, ALU.max, ALU.mult).then_inc(w_ready, 1)

            def add_up(g, q, d, n, k):
                I, J = group_of(g, q, d)
                dve.wait_ge(w_used, GR * n + 2 * GR)
                for h in range(2):
                    rows_h = attended[:, bass.ds(GR * I + 2 * h, 2), :].rearrange("p t d -> p (t d)")
                    last = V.tensor_tensor(rows_h, rows_h, p_att[h][:, 0:2 * D1], ALU.add)
                last.then_inc(att_added, 1)

            def attend(g, q, after=None, lo=0):
                def one(d, n, k):
                    weigh(g, q, d, n, k)
                    add_up(g, q, d, n, k)
                    if after:
                        dve.drain()
                        after(d)
                if lo == 0 and not (isinstance(g, int) and lump(g, q)[1] == 0):
                    attend_in(g, q)
                part(dve, g, q, lo, LUMP, one)

            def just(g, q, k, body):
                part(dve, g, q, k, k + 1, lambda d, n, k: body(g, q, d, n, k))

            for q in range(GR):
                find(q, q % 2)
                lists(q, q % 2)
                if q:
                    reduce(q - 1, (q - 1) % 2)
                    dve.drain()
                    moments(q - 1, q - 1)
            dve.wait_ge(norm_done, 1)

            def step(g, q):
                t = GR * (g + 1) + q
                now = due(g, q)
                if q == 1:
                    wait(std_ready, XC + g + 1)
                    scale_and_shift(slice(0, GR)).then_inc(shift_ready, 1)
                find(t, q % 2)
                if now and isinstance(now[0], int) and lump(*now)[1] == 0:
                    now = None
                if now:
                    attend_in(*now)
                    just(*now, 0, weigh)
                lists(t, q % 2)
                if now:
                    just(*now, 0, add_up)
                    just(*now, 1, weigh)
                reduce(t - 1, (q + 1) % 2)
                if now:
                    just(*now, 1, add_up)
                dve.drain()
                moments(t - 1, (q - 1) % GR)
                if q == 0:
                    variance(slice(0, GR)).then_inc(var_ready, 1)
                if now:
                    attend(*now, lo=2)

            over_groups(dve, step)
            for q in range(1, GR):
                attend(NG - 2, q)
            reduce(T - 1, 1)
            dve.drain()
            moments(T - 1, GR - 1)
            variance(slice(0, GR)).then_inc(var_ready, 1)
            dve.wait_ge(std_ready, XC + NG)
            scale_and_shift(slice(0, GR)).then_inc(shift_ready, 1)

            def divide(I):
                b = I % 2
                tiles = slice(GR * I, GR * (I + 1))
                then(V.tensor_scalar(rden[:, tiles], attended[:, tiles, D:D1].rearrange("p t o -> p (t o)"), LEAST_DEN, None, ALU.max))
                then(V.reciprocal(rden[:, tiles], rden[:, tiles]))
                if I >= 2:
                    dve.wait_ge(out_stored[b], 16 * (I // 2))
                then(V.tensor_tensor(elu_pos(b), attended[:, tiles, 0:D], rden[:, tiles].unsqueeze(2).to_broadcast([P, GR, D]), ALU.mult))
                V.tensor_scalar(elu_neg(b), elu_pos(b), 0.0, None, ALU.min).then_inc(elu_in, 1)
                then(V.scalar_tensor_tensor(elu_pos(b), elu_pos(b), 0.0, x_sb[:, tiles, :], ALU.max, ALU.add))

            def finish(I):
                b = I % 2
                dve.wait_ge(elu_exp, I + 1)
                V.scalar_tensor_tensor(elu_out(b), elu_e(b), -1.0, elu_pos(b), ALU.add, ALU.add).then_inc(out_ready, 1)

            def after(I):
                if I < NG - 1:
                    divide(I)
                if 0 < I:
                    finish(I - 1)
            attend(NG - 1, 0, after)
            attend(NG - 1, 1, after)
            attend(NG - 1, 2)
            attend(NG - 1, 3)
            dve.drain()
            divide(NG - 1)
            dens = attended[:, :, D:D1].rearrange("p t o -> p (t o)")
            V.tensor_scalar(rden[:], dens, LEAST_DEN, None, ALU.is_ge)
            V.tensor_scalar(lam[:], dens, MOST_DEN, None, ALU.is_le)
            dve.drain()
            then(V.tensor_tensor(rden[:], rden[:], lam[:], ALU.mult))
            then(V.tensor_reduce(lost_row[:, 1:2], rden[:], axis=X, op=ALU.add))
            then(V.tensor_reduce(lost_row[:, 0:1], lost[:].rearrange("p k t -> p (k t)"), axis=X, op=ALU.max))
            then(V.tensor_scalar(lost_row[:, 1:2], lost_row[:, 1:2], float(T), None, ALU.not_equal))
            V.tensor_tensor(lost_row[:, 0:1], lost_row[:, 0:1], lost_row[:, 1:2], ALU.add).then_inc(lost_ready, 1)
            finish(NG - 1)
            dve.wait_ge(lost_sum, 1)
            V.tensor_scalar(redo[:], p_small[0:1, 0:1], 0.5, None, ALU.is_gt).then_inc(redo_known, 1)
            dve.wait_ge(redo_known, 1)

            with dve.If(dve.value_load(redo[0:1, 0:1], min_val=0, max_val=1)):
                dve.sem_inc(back_tile, 1)
                dve.sem_inc(back_used, 2)
                with dve.Fori(0, T) as t:
                    acc = nbr_max[:, bass.ds(t, 1), :].rearrange("p t d -> p (t d)")
                    dve.wait_ge(back_adj, 16 * (t + 1))
                    V.tensor_scalar(key, adj_t[:, 0], 0, None, ALU.not_equal).then_inc(back_tile, 1)
                    V.tensor_scalar(acc, ones[:], 0.0, None, ALU.mult)
                    dve.drain()
                    with dve.Fori(0, CH // 2) as c:
                        for b in range(2):
                            dve.wait_ge(back_h[b], t * (16 * CH // 2) + 16 * c + 16)
                            for r in range(T):
                                j = (2 * c + b) * T + r
                                then(V.scalar_tensor_tensor(acc, G[:, b, r, :], key[:, bass.ds(j, 1)], acc, ALU.mult, ALU.max))
                            dve.sem_inc(back_used, 1)
                dve.wait_ge(x_again, 16 * XC)
                then(V.tensor_tensor(x_sb[:], x_sb[:], nbr_max, ALU.add))
                for c in range(XC):
                    for t in range(XT):
                        V.bn_stats(stats[:, t, :], x_sb[:, c * XT + t, :])
                    dve.drain()
                    for t in range(XT):
                        V.bn_aggr(mv[:, c * XT + t, :], stats[:, t, :])
                    dve.drain()
                variance(slice(0, T)).then_inc(var2_ready, 1)
                dve.wait_ge(std2_ready, 1)
                then(scale_and_shift(slice(0, T)))
                with dve.Fori(0, T) as t:
                    V.tensor_scalar(h_sb[:, bass.ds(t, 1), :], x_sb[:, bass.ds(t, 1), :], rstd[:, bass.ds(t, 1)],
                                    shift[:, bass.ds(t, 1)], ALU.mult, ALU.add)
                dve.drain()
                V.tensor_scalar(h_sb, h_sb, 0.0, None, ALU.max).then_inc(h2_all, 1)
                dve.wait_ge(W_copied, T)

                def attend_row(i, b, first):
                    t = 2 * i + b
                    dve.wait_ge(adj2_in[b], 16 * (i + 1))
                    if not first:
                        dve.wait_ge(eT_ready, t * (T // 4))
                    Z = G0.rearrange("p k d -> p (k d)")
                    F = G1.rearrange("p k d -> p (k d)")
                    then(V.tensor_scalar(Z, r_all[:], s_col[:, bass.ds(t, 1)], None, ALU.add))
                    then(V.scalar_tensor_tensor(Z, Z, ALPHA, Z, ALU.mult, ALU.max))
                    then(V.tensor_scalar(F, adj_t[:, b], 0, -2.0 * NEG_FILL, ALU.is_gt, ALU.mult).then_inc(adj2_used, 1))
                    then(V.scalar_tensor_tensor(Z, F, NEG_FILL, Z, ALU.add, ALU.min))
                    V.tensor_reduce(neg_max[:, b:b + 1], Z, axis=X, op=ALU.max, negate=True).then_inc(z_ready, 1)
                    dve.wait_ge(av_ready, t + 1)
                    then(V.reciprocal(rden[:, b:b + 1], den[:, b:b + 1]))
                    then(V.tensor_scalar(hp[:], p_att[b][:, 0:D], rden[:, b:b + 1], None, ALU.mult))
                    V.tensor_scalar(hm[:], hp[:], 0.0, None, ALU.min).then_inc(hm_ready, 1)
                    if not first:
                        dve.wait_ge(stored[b], 16 * i)
                    then(V.scalar_tensor_tensor(hp[:], hp[:], 0.0, x_sb[:, bass.ds(t, 1), :].rearrange("p t d -> p (t d)"), ALU.max, ALU.add))
                    dve.wait_ge(he_ready, t + 1)
                    V.scalar_tensor_tensor(res[:, b], he[:], -1.0, hp[:], ALU.add, ALU.add).then_inc(res_ready, 1)

                attend_row(0, 0, True)
                dve.wait_ge(eT_ready, T // 4)
                attend_row(0, 1, True)
                with dve.Fori(1, T // 2) as i:
                    for b in range(2):
                        attend_row(i, b, False)


_INS = ["x", "adj", "L1_gnn_W", "L1_gnn_a"]


def kernel(**inputs):
    import numpy as np
    import concourse.bacc as bacc
    from concourse import mybir as mb
    from concourse.bass_utils import run_bass_kernel_spmd as run

    nc = bacc.Bacc("TRN2", target_bir_lowering=False, num_devices=1)
    arrays, args = {}, []
    for name in _INS:
        arr = np.ascontiguousarray(inputs[name])
        arrays[f"in_{name}"] = arr
        args.append(nc.dram_tensor(f"in_{name}", arr.shape, mb.dt.from_np(arr.dtype), kind="ExternalInput").ap())
    shape = inputs["x"].shape
    out = nc.dram_tensor("out", shape, mb.dt.float32, kind="ExternalOutput").ap()
    gnn_layers(nc, *args, out)
    r = run(nc, [arrays], core_ids=[0])
    return r.results[0]["out"]
```

```python
from contextlib import ExitStack

import concourse.bass as bass
from concourse import mybir
from concourse.alu_op_type import AluOpType as ALU

F32 = mybir.dt.float32
BF16 = mybir.dt.bfloat16
FP8 = mybir.dt.float8e4
U8 = mybir.dt.uint8
I32 = mybir.dt.int32
U32 = mybir.dt.uint32
ACT = mybir.ActivationFunctionType
X = mybir.AxisListType.X

P = 128
TOP = 8
SLOTS = 40
OFTEN = (32, 28, 22, 20)
SURE = 8
GR = 4
EPS = 1e-5
ALPHA = 0.2
REST = 1.0 - ALPHA
NEG_FILL = -9000000000000000.0
SLACK = 1.001
LEAST_DEN = 1e-18
MOST_DEN = 1e30


def gnn_layers(nc, x, adj, W, a, out):
    N, D = x.shape
    T = N // P
    NG = T // GR
    GP = GR * P
    CAND = T * TOP
    KC = 512 // P
    NK = T // KC
    TB = 1024 // P
    NT = T // TB
    D1 = D + 1
    XC = 4
    XT = T // XC
    AHEAD = GR * NG
    LUMP = (NG + 1) // 2
    assert len(OFTEN) == GR == 4

    ctx = ExitStack()
    with ctx:
        def sb(name, shape, dt=F32):
            return ctx.enter_context(nc.sbuf_tensor(name, shape, dt))

        def ps(name, shape, dt=F32):
            return ctx.enter_context(nc.psum_tensor(name, shape, dt))

        def sem(name):
            return ctx.enter_context(nc.semaphore(name))

        h_rows = nc.dram_tensor("h_rows", [N, D], F32, kind="Internal").ap()
        maskT_rows = nc.dram_tensor("maskT_rows", [T, P, T, P], U8, kind="Internal").ap()

        adj_t = sb("adj_t", [P, 2, N], I32)
        x_sb = sb("x_sb", [P, T, D])
        G = sb("G", [P, 2, SLOTS, D])
        attended = sb("attended", [P, T, D1])
        Whg = sb("Whg", [P, T, D1])
        r_all = sb("r_all", [P, N])
        blocks = sb("blocks", [P, GR * GP + 2 * LUMP * GR * GP // 4])
        masks = sb("masks", [P, N])
        weights = blocks[:, 0:GR * GP].rearrange("p (j i) -> p j i", j=GR)
        M = blocks[:, GR * GP:].bitcast(U8).rearrange("p (b n i q) -> p b n i q", b=2, n=LUMP, i=GR)
        h_sb = blocks[:, 0:N].rearrange("p (t d) -> p t d", t=T)
        sign = masks[:, 0:N // 2].bitcast(BF16)
        maskT = masks[:, N // 2:].bitcast(FP8).rearrange("p (b t i) -> p b t i", b=2, t=T)
        mask_bytes = masks[:, N // 2:].bitcast(U8).rearrange("p (b t i) -> p b t i", b=2, t=T)
        assert GR * GP * 4 + 2 * LUMP * GR * GP <= blocks[:].free_nbytes()

        cand = sb("cand", [P, CAND])
        nbrs = sb("nbrs", [P, GR, SLOTS])
        ranked = sb("ranked", [P, GR, SLOTS])
        idx = sb("idx", [P, GR, SLOTS], U32)
        junk = sb("junk", [P, SLOTS])
        degree = sb("degree", [P, GR])
        ranked_degree = sb("ranked_degree", [P, GR])
        tie_broken = sb("tie_broken", [P, GR])
        place = sb("place", [P, GR])
        rank = sb("rank", [P, GR])
        is_rank = sb("is_rank", [P, GR, GR])
        is_rank_next = sb("is_rank_next", [P, GR, GR])
        of_rank = sb("of_rank", [P, GR, GR])
        sign_sum = sb("sign_sum", [P, 2])
        lost = sb("lost", [P, 2, T])
        lost_row = sb("lost_row", [P, 2])
        n_slots = sb("n_slots", [1, GR], I32)
        landed_i = sb("landed_i", [1, GR], I32)
        deg_max = sb("deg_max", [1, GR])
        redo = sb("redo", [1, 1], I32)
        nbr_rows = sb("nbr_rows", [P, GR, D])
        more_row = sb("more_row", [P, D])
        stats = sb("stats", [P, XT, 6])
        mv = sb("mv", [P, T, 2])
        rstd = sb("rstd", [P, T])
        shift = sb("shift", [P, T])
        h2 = sb("h2", [P, GR, D])
        h2T_g = sb("h2T_g", [P, GP])
        WhT_g = sb("WhT_g", [P, GP])
        lam = sb("lam", [P, T])
        g_col = sb("g_col", [P, T])
        ident = sb("ident", [P, P])
        ident_b = sb("ident_b", [P, P], BF16)
        down_b = sb("down_b", [P, P], BF16)
        seg_b = sb("seg_b", [P, T, P], BF16)
        ones = sb("ones", [P, P])
        W_sb = sb("W_sb", [D, D])
        WT_sb = sb("WT_sb", [D, D])
        a_sb = sb("a_sb", [D, 2])
        a1_all = sb("a1_all", [D, P])
        a2_all = sb("a2_all", [D, P])
        Wa = sb("Wa", [D, 2])
        bound = sb("bound", [P, 2])
        r_bias = sb("r_bias", [P, 1])
        g_bias = sb("g_bias", [P, 1])
        rden = sb("rden", [P, T])
        neg_rden = sb("neg_rden", [P, T])
        s_col = sb("s_col", [P, T])
        neg_max = sb("neg_max", [P, 2])
        den = sb("den", [P, 2])
        hp = sb("hp", [P, D])
        hm = sb("hm", [P, D])
        he = sb("he", [P, D])
        res = sb("res", [P, 2, D])
        G0 = G[:, 0, 0:T, :]
        G1 = G[:, 1, 0:T, :]
        key = masks[:]
        nbr_max = attended[:].rearrange("p t d -> p (t d)")[:, 0:N].rearrange("p (t d) -> p t d", t=T)
        Wh = Whg[:].rearrange("p t d -> p (t d)")[:, 0:N].rearrange("p (t d) -> p t d", t=T)
        h2T = key
        WhT = adj_t[:, 1].bitcast(F32)

        p_T = [ps(f"p_T{i}", [P, 1024], BF16) for i in range(2)]
        p_key = [ps(f"p_key{i}", [P, 512]) for i in range(2)]
        p_att = [ps(f"p_att{i}", [P, 512]) for i in range(2)]
        key_banks = [p_key[0][:], p_key[1][:], p_T[0][:].bitcast(F32), p_T[1][:].bitcast(F32)]
        KB = len(key_banks)
        p_grp = ps("p_grp", [P, 512])
        p_small = ps("p_small", [P, 512])

        x_in = [sem(f"x_in{c}") for c in range(XC)]
        w_in = sem("w_in")
        consts = sem("consts")
        WT_ready = sem("WT_ready")
        WT_copied = sem("WT_copied")
        Wa_ready = sem("Wa_ready")
        Wa_sq = sem("Wa_sq")
        norm_ready = sem("norm_ready")
        bound_ready = sem("bound_ready")
        bias_ready = sem("bias_ready")
        var_ready = sem("var_ready")
        std_ready = sem("std_ready")
        h_ready = sem("h_ready")
        h_stored = sem("h_stored")
        adj_in = [sem(f"adj_in{b}") for b in range(2)]
        sign_ready = sem("sign_ready")
        T_ready = sem("T_ready")
        T_copied = sem("T_copied")
        mask_stored = [sem(f"mask_stored{b}") for b in range(2)]
        key_ready = sem("key_ready")
        key_used = sem("key_used")
        passed = sem("passed")
        act_passed = sem("act_passed")
        pe_passed = sem("pe_passed")
        sp_passed = sem("sp_passed")
        deg_ready = sem("deg_ready")
        slots_known = sem("slots_known")
        listed = sem("listed")
        degT_ready = sem("degT_ready")
        lists_ready = sem("lists_ready")
        zeroed = sem("zeroed")
        turn = sem("turn")
        gathered = [sem(f"gathered{b}") for b in range(2)]
        reduced = sem("reduced")
        shift_ready = sem("shift_ready")
        h2_ready = sem("h2_ready")
        grp_mm = sem("grp_mm")
        grp_copied = sem("grp_copied")
        M_in = [sem(f"M_in{b}") for b in range(2)]
        w_ready = sem("w_ready")
        w_used = sem("w_used")
        att_added = sem("att_added")
        divisor_ready = sem("divisor_ready")
        elu_exp = sem("elu_exp")
        out_ready = sem("out_ready")
        out_stored = [sem(f"out_stored{b}") for b in range(2)]
        lost_ready = sem("lost_ready")
        lost_sum = sem("lost_sum")
        redo_known = sem("redo_known")
        x_again = sem("x_again")
        back_adj = sem("back_adj")
        back_h = [sem(f"back_h{b}") for b in range(2)]
        back_used = sem("back_used")
        back_tile = sem("back_tile")
        var2_ready = sem("var2_ready")
        std2_ready = sem("std2_ready")
        h2_all = sem("h2_all")
        hT_ready = sem("hT_ready")
        hT_copied = sem("hT_copied")
        W_mm = sem("W_mm")
        W_copied = sem("W_copied")
        adj2_in = [sem(f"adj2_in{b}") for b in range(2)]
        adj2_used = sem("adj2_used")
        z_ready = sem("z_ready")
        e_ready = sem("e_ready")
        eT_ready = sem("eT_ready")
        eT_copied = sem("eT_copied")
        av_ready = sem("av_ready")
        hm_ready = sem("hm_ready")
        he_ready = sem("he_ready")
        res_ready = sem("res_ready")
        stored = [sem(f"stored{b}") for b in range(2)]
        block = ctx.enter_context(nc.Block())

        rows = lambda v: v.rearrange("(t p) d -> p t d", p=P)
        adj_tiles = adj.rearrange("(t p) j -> t p j", p=P)
        out_tiles = out.rearrange("(t p) d -> t p d", p=P)
        out_groups = out.rearrange("(g q p) d -> g p q d", q=GR, p=P)
        h_chunks = h_rows.rearrange("(c r) d -> c (r d)", r=T)
        CH = N // T

        def lump(g, q):
            if q == 0:
                return 0, (g + 1) // 2, g * g, (g * g + 1) // 2
            if q == 1:
                return (g + 1) // 2, g // 2 + 1, g * g + (g + 1) // 2, ((g + 1) * (g + 1) + 1) // 2
            if q == 2:
                return 0, g // 2, g * g + g + 1, (g * g + g) // 2
            return g // 2, (g + 1) // 2, g * g + g + 1 + g // 2, ((g + 1) * (g + 2)) // 2

        def due(g, q):
            of, which = (g - 1, 0) if q == GR - 1 else (g - 2, q + 1)
            return None if isinstance(g, int) and of < 0 else (of, which)

        def group_of(g, q, d):
            return (d, g) if q < 2 else (g, d)

        def part(eng, g, q, lo, hi, body):
            first, n, number, _ = lump(g, q)
            if isinstance(g, int):
                for k in range(lo, min(hi, n)):
                    body(first + k, number + k, k)
                return
            most = lump(NG - 3 if q == 0 else NG - 4, q)[1]
            if lo >= most:
                return
            if hi - lo == 1:
                with eng.If(n > lo):
                    body(first + lo, number + lo, lo)
            else:
                with eng.If(n > lo), eng.Fori(lo, n) as k:
                    body(first + k, number + k, k)

        def over_groups(eng, step):
            for g in range(2):
                for q in range(GR):
                    step(g, q)
            with eng.Fori(2, NG - 1) as g:
                for q in range(GR):
                    step(g, q)

        def in_range(t):
            return t if isinstance(t, int) else nc.s_assert_within(
                t, 0, T - 1, skip_runtime_bounds_check_because="inside unless_last for the last group")

        def unless_last(eng, g, body):
            if isinstance(g, int):
                body()
            else:
                with eng.If(g < NG - 2):
                    body()

        FIRST_LAST = lump(NG - 3, 1)[2]

        def pair_of(n):
            return (p_att, p_key)[(n - FIRST_LAST) % 2]

        def elu_pos(b):
            return G[:, b, 0:GR, :]

        def elu_neg(b):
            return G[:, b, GR:2 * GR, :]

        def elu_e(b):
            return G[:, b, 2 * GR:3 * GR, :]

        def elu_out(b):
            return G[:, b, 3 * GR:4 * GR, :]

        @block.sync
        def _(sp):
            sp.dma_start(adj_t[:, 0], adj_tiles[0]).then_inc(adj_in[0], 16)
            for c in range(XC):
                sp.dma_start(x_sb[:, c * XT:(c + 1) * XT], rows(x)[:, c * XT:(c + 1) * XT]).then_inc(x_in[c], 16)
            sp.dma_start(adj_t[:, 1], adj_tiles[1]).then_inc(adj_in[1], 16)
            sp.dma_start(W_sb[:], W).then_inc(w_in, 16)
            for k in range(2):
                sp.dma_start(a_sb[:, k:k + 1], a[k * D:(k + 1) * D, :]).then_inc(w_in, 16)
            for c in range(XC):
                sp.wait_ge(h_ready, c + 1)
                sp.dma_start(rows(h_rows)[:, c * XT:(c + 1) * XT], h_sb[:, c * XT:(c + 1) * XT]).then_inc(h_stored, 16)

            def load_adj(t, q):
                sp.wait_ge(sign_ready, t + 1)
                sp.dma_start(adj_t[:, q % 2], adj_tiles[in_range(t + 2)]).then_inc(adj_in[q % 2], 16)

            def store_mask(t, q):
                sp.wait_ge(T_copied, NT * (t + 1))
                sp.sem_inc(sp_passed, 1)
                sp.dma_start(maskT_rows[t], mask_bytes[:, q % 2]).then_inc(mask_stored[q % 2], 16)

            def load_lump(g, q):
                if q == 0:
                    for k in range(2):
                        sp.wait_ge(mask_stored[k], 16 * (GR // 2) * (g + 1))
                if isinstance(g, int) and lump(g, q)[1] == 0:
                    return
                b = q % 2

                def one(d, n, k):
                    I, J = group_of(g, q, d)
                    sp.dma_start(M[:, b, k] if isinstance(k, int) else M[:, b, bass.ds(k, 1)].rearrange("p n i q -> p (n i) q"),
                                 maskT_rows.rearrange("(I i) p (J j) r -> I J p i (j r)", i=GR, j=GR)[I, J])\
                        .then_inc(M_in[b], 16)

                read = ((g * (2 * g - 1) + 1) // 2, g * g, g * g + (g + 1) // 2, g * g + g + 1)[q]
                sp.wait_ge(w_ready, AHEAD + GR * read)
                sp.sem_inc(sp_passed, 1)
                part(sp, g, q, 0, LUMP, one)

            def step(g, q):
                t = GR * (g + 1) + q
                if q < 2:
                    load_adj(t, q)
                else:
                    unless_last(sp, g, lambda: load_adj(t, q))
                store_mask(t, q)
                of, which = (g - 1, q - 2) if q >= 2 else (g - 2, q + 2)
                if not (isinstance(g, int) and of < 0):
                    load_lump(of, which)

            for q in range(GR):
                load_adj(q, q)
                store_mask(q, q)
            over_groups(sp, step)

            def store_out(g, b):
                sp.wait_ge(out_ready, g + 1)
                sp.dma_start(out_groups[g], elu_out(b)).then_inc(out_stored[b], 16)
            for g, q in ((NG - 3, 2), (NG - 3, 3), (NG - 2, 0), (NG - 2, 1), (NG - 2, 2), (NG - 2, 3)):
                load_lump(g, q)
            for q, groups in enumerate(((), (0, 1), (2, 3, 4), (5, 6, 7))):
                load_lump(NG - 1, q)
                for g in groups:
                    store_out(g, g % 2)
            for b in range(2):
                sp.wait_ge(out_stored[b], 16 * NG // 2)

            sp.wait_ge(redo_known, 1)
            with sp.If(sp.value_load(redo[0:1, 0:1], min_val=0, max_val=1)):
                for c in range(XC):
                    sp.dma_start(x_sb[:, c * XT:(c + 1) * XT], rows(x)[:, c * XT:(c + 1) * XT]).then_inc(x_again, 16)
                with sp.Fori(0, T) as t:
                    sp.wait_ge(back_tile, t + 1)
                    sp.dma_start(adj_t[:, 0], adj_tiles[t]).then_inc(back_adj, 16)
                    with sp.Fori(0, CH // 2) as c:
                        for b in range(2):
                            sp.wait_ge(back_used, t * CH + 2 * c + b + 1)
                            sp.dma_start(G[:, b, 0:T, :].rearrange("p r d -> p (r d)"),
                                         h_chunks[2 * c + b].partition_broadcast(P)).then_inc(back_h[b], 16)
                sp.wait_ge(W_copied, T)
                for b in range(2):
                    sp.dma_start(adj_t[:, b], adj_tiles[b]).then_inc(adj2_in[b], 16)
                with sp.Fori(1, T // 2) as i:
                    for b in range(2):
                        sp.wait_ge(adj2_used, 2 * i + b - 1)
                        sp.dma_start(adj_t[:, b], adj_tiles[2 * i + b]).then_inc(adj2_in[b], 16)
                        sp.wait_ge(res_ready, 2 * i + b - 1)
                        sp.dma_start(out_tiles[2 * i + b - 2], res[:, b]).then_inc(stored[b], 16)
                for b in range(2):
                    sp.wait_ge(res_ready, T - 1 + b)
                    sp.dma_start(out_tiles[T - 2 + b], res[:, b]).then_inc(stored[b], 16)
                for b in range(2):
                    sp.wait_ge(stored[b], 16 * (T // 2))

        @block.gpsimd
        def _(pool):
            pool.memset(ones[:], 1.0).then_inc(consts, 1)
            pool.iota(down_b[:], [[0, P]], base=P, channel_multiplier=-1,
                      allow_small_or_imprecise_dtypes=True).then_inc(consts, 1)
            pool.wait_ge(consts, 2)
            for m, src in ((ident_b, ones), (ident, ones), (down_b, down_b)):
                pool.affine_select(out=m[:], in_=src[:], compare_op=ALU.is_equal, fill=0.0,
                                   base=0, pattern=[[-1, P]], channel_multiplier=1).then_inc(consts, 1)
            pool.iota(seg_b[:], [[-P, T], [0, P]], base=N - P, channel_multiplier=0,
                      allow_small_or_imprecise_dtypes=True).then_inc(consts, 1)
            pool.wait_ge(consts, 6)
            pool.affine_select(out=seg_b[:], in_=seg_b[:], compare_op=ALU.is_equal, fill=0.0,
                               base=0, pattern=[[0, T], [-1, P]], channel_multiplier=1).then_inc(consts, 1)
            pool.memset(G[:], 0.0).then_inc(consts, 1)
            pool.memset(attended[:], 0.0).then_inc(consts, 1)
            pool.wait_ge(consts, 9)
            pool.wait_ge(h_stored, 16 * XC)

            def gather(q, k):
                pool.indirect_dma_start(
                    G[:, q % 2, k, :], None, h_rows, bass.IndirectOffsetOnAxis(ap=idx[:, q, k:k + 1], axis=0),
                    bounds_check=N - 1, oob_is_err=False).then_inc(gathered[q % 2], 16)

            def gather_while(q, k, n):
                with pool.If(n > k):
                    gather(q, k)
                    if k + 1 < SLOTS:
                        gather_while(q, k + 1, n)

            with pool.Fori(0, NG) as g:
                for q in range(GR):
                    pool.wait_ge(lists_ready, GR * g + q + 1)
                    pool.wait_ge(zeroed, GR * g + q + 1)
                    pool.sem_inc(turn, 1)
                    n = pool.value_load(n_slots[0:1, q:q + 1], min_val=0, max_val=SLOTS)
                    for k in range(SURE):
                        gather(q, k)
                    gather_while(q, SURE, n)

            for g in range(NG):
                b = g % 2
                pool.wait_ge(elu_exp, g + 1)
                pool.tensor_tensor(elu_pos(b), elu_pos(b), x_sb[:, GR * g:GR * (g + 1), :], ALU.add)
                pool.tensor_tensor(elu_e(b), elu_e(b), ones[:].unsqueeze(1).to_broadcast([P, GR, D]), ALU.subtract)
                if g >= 2:
                    pool.wait_ge(out_stored[b], 16 * (g // 2))
                pool.drain()
                pool.tensor_tensor(elu_out(b), elu_e(b), elu_pos(b), ALU.add).then_inc(out_ready, 1)

        @block.scalar
        def _(act):
            def wait(s, value):
                act.wait_ge(s, value)
                act.sem_inc(act_passed, 1)

            def take_sign(t, b, turn2):
                if not (isinstance(t, int) and t < 2):
                    wait(listed, t - 1)
                act.wait_ge(adj_in[b], 16 * (turn2 + 1))
                if not (isinstance(t, int) and t == 0):
                    act.wait_ge(T_ready, NT * t)
                act.activation(sign, adj_t[:, b], ACT.Sign, accum_out=sign_sum[:, b:b + 1]).then_inc(sign_ready, 1)

            def mask(t, b, turn2):
                if not (isinstance(t, int) and t < 2):
                    act.wait_ge(mask_stored[b], 16 * turn2)
                    act.wait_ge(key_ready, NK * (t - 1))
                for k in range(NT):
                    wait(T_ready, NT * t + k + 1)
                    act.activation(maskT[:, b, k * TB:(k + 1) * TB, :], p_T[k % 2][:], ACT.Relu, saturate=False).then_inc(T_copied, 1)

            def zero(t, b):
                act.wait_ge(reduced, t - 1)
                act.memzero(G[:, b]).then_inc(zeroed, 1)

            def norm(g):
                act.wait_ge(var_ready, g + 2)
                act.activation(rstd[:, 0:GR], rstd[:, 0:GR], ACT.Sqrt).then_inc(std_ready, 1)
                act.wait_ge(shift_ready, g + 2)
                for q in range(GR):
                    last = act.activation(h2[:, q, :], x_sb[:, bass.ds(GR * g + q, 1), :].rearrange("p t d -> p (t d)"),
                                          ACT.Relu, bias=shift[:, q:q + 1], scale=rstd[:, q:q + 1])
                last.then_inc(h2_ready, 1)

            def copy_group(g):
                act.wait_ge(grp_mm, 4 * g + 1)
                act.activation(h2T_g[:], p_grp[:], ACT.Copy).then_inc(grp_copied, 1)
                act.wait_ge(grp_mm, 4 * g + 2)
                act.activation(WhT_g[:], p_grp[:], ACT.Copy).then_inc(grp_copied, 1)

            def weigh_group(g):
                tiles = bass.ds(GR * g, GR)
                act.wait_ge(grp_mm, 4 * g + 3)
                act.activation(r_all[:, bass.ds(GP * g, GP)], p_grp[:], ACT.Exp, bias=r_bias[:], scale=REST)
                act.activation(lam[:, tiles], p_small[:, P:P + GR], ACT.Exp, bias=r_bias[:], scale=-REST)
                act.activation(g_col[:, tiles], p_small[:, P:P + GR], ACT.Exp, bias=g_bias[:]).then_inc(grp_copied, 1)
                wait(grp_mm, 4 * g + 4)
                act.drain()
                for q in range(GR):
                    t = bass.ds(GR * g + q, 1)
                    act.activation(Whg[:, t, 0:D].rearrange("p t d -> p (t d)"), p_grp[:, q * P:(q + 1) * P], ACT.Copy,
                                   scale=g_col[:, t])
                act.activation(Whg[:, tiles, D:D1].rearrange("p t o -> p (t o)"), g_col[:, tiles], ACT.Copy).then_inc(grp_copied, 1)

            act.sem_inc(zeroed, 2)
            take_sign(0, 0, 0)
            mask(0, 0, 0)
            act.wait_ge(var_ready, 1)
            act.activation(rstd[:], rstd[:], ACT.Sqrt).then_inc(std_ready, 1)
            act.wait_ge(shift_ready, 1)
            for t in range(T):
                last = act.activation(h_sb[:, t, :], x_sb[:, t, :], ACT.Relu, bias=shift[:, t:t + 1], scale=rstd[:, t:t + 1])
                if (t + 1) % XT == 0:
                    last.then_inc(h_ready, 1)
            take_sign(1, 1, 0)
            mask(1, 1, 0)
            act.wait_ge(WT_ready, 1)
            act.activation(WT_sb[:], p_grp[:, 0:D], ACT.Copy).then_inc(WT_copied, 1)
            act.wait_ge(norm_ready, 1)
            act.activation(bound[:], p_small[:, 0:2], ACT.Sqrt, scale=float(D)).then_inc(bound_ready, 1)
            for q in range(2, GR):
                take_sign(q, q % 2, q // 2)
                mask(q, q % 2, q // 2)
            act.wait_ge(bias_ready, 1)

            def step(g, q):
                t = GR * (g + 1) + q
                if q < 3:
                    take_sign(t, q % 2, 2 * (g + 1) + q // 2)
                mask(t, q % 2, 2 * (g + 1) + q // 2)
                done = not (isinstance(g, int) and g == 0)
                if q == 3 and done:
                    weigh_group(g - 1)
                if done:
                    zero(GR * g + q, q % 2)
                elif q % 2 == 0:
                    zero(2 + q // 2, q // 2)
                if q == 1 and done:
                    norm(g - 1)
                if q == 2:
                    take_sign(t + 1, 1, 2 * (g + 1) + 1)
                    if done:
                        copy_group(g - 1)

            over_groups(act, step)
            zero(T - 4, 0)
            zero(T - 3, 1)
            norm(NG - 2)
            copy_group(NG - 2)
            weigh_group(NG - 2)
            zero(T - 2, 0)
            zero(T - 1, 1)
            norm(NG - 1)
            copy_group(NG - 1)
            weigh_group(NG - 1)
            for g in range(NG):
                b = g % 2
                act.wait_ge(divisor_ready, g + 1)
                if g >= 2:
                    act.wait_ge(out_ready, g - 1)
                for q in range(GR):
                    t = GR * g + q
                    act.activation(elu_neg(b)[:, q, :], attended[:, t, 0:D], ACT.Relu, scale=neg_rden[:, t:t + 1])
                for q in range(GR):
                    t = GR * g + q
                    act.activation(elu_pos(b)[:, q, :], attended[:, t, 0:D], ACT.Relu, scale=rden[:, t:t + 1])
                act.drain()
                act.activation(elu_e(b), elu_neg(b), ACT.Exp, scale=-1.0).then_inc(elu_exp, 1)

            act.wait_ge(redo_known, 1)
            with act.If(act.value_load(redo[0:1, 0:1], min_val=0, max_val=1)):
                act.wait_ge(var2_ready, 1)
                act.activation(rstd[:], rstd[:], ACT.Sqrt).then_inc(std2_ready, 1)
                for g in range(T // 4):
                    act.wait_ge(hT_ready, g + 1)
                    act.activation(h2T[:, g * 512:(g + 1) * 512], p_key[g % 2][:], ACT.Copy).then_inc(hT_copied, 1)
                for g in range(T // 4):
                    act.wait_ge(W_mm, 3 * g + 1)
                    act.activation(WhT[:, g * 512:(g + 1) * 512], p_att[0][:], ACT.Copy).then_inc(W_copied, 1)
                    act.wait_ge(W_mm, 3 * g + 2)
                    act.activation(Wh[:, 4 * g:4 * g + 4, :], p_att[1][:], ACT.Copy).then_inc(W_copied, 1)
                    act.wait_ge(W_mm, 3 * g + 3)
                    act.activation(r_all[:, g * 512:(g + 1) * 512], p_key[0][:], ACT.Copy).then_inc(W_copied, 1)
                    act.activation(s_col[:, 4 * g:4 * g + 4], p_small[:, 8:12], ACT.Copy).then_inc(W_copied, 1)
                with act.Fori(0, T // 2) as i:
                    for b in range(2):
                        t = 2 * i + b
                        act.wait_ge(z_ready, t + 1)
                        act.activation(G0, G0, ACT.Exp, bias=neg_max[:, b:b + 1], accum_out=den[:, b:b + 1]).then_inc(e_ready, 1)
                        for g in range(T // 4):
                            act.wait_ge(eT_ready, t * (T // 4) + g + 1)
                            act.activation(h_sb[:, 4 * g:4 * g + 4, :], p_key[g % 2][:], ACT.Copy).then_inc(eT_copied, 1)
                        act.wait_ge(hm_ready, t + 1)
                        act.activation(he[:], hm[:], ACT.Exp).then_inc(he_ready, 1)

        @block.tensor
        def _(pe):
            def transposes(t):
                if not (isinstance(t, int) and t == 0):
                    pe.wait_ge(key_used, NK * t)
                    pe.sem_inc(pe_passed, 1)
                pe.wait_ge(sign_ready, t + 1)
                for k in range(NT):
                    if not (isinstance(t, int) and NT * t + k < 2):
                        pe.wait_ge(T_copied, NT * t + k - 1)
                    for s in range(TB):
                        j = k * TB + s
                        last = pe.transpose(p_T[k % 2][:, s * P:(s + 1) * P], sign[:, j * P:(j + 1) * P], ident_b[:])
                    last.then_inc(T_ready, 1)

            def keys(t, b):
                for c in range(NK):
                    copied = c * KC // TB + 1
                    if 2 <= c < KB:
                        copied = NT - KB + c + 1
                    pe.wait_ge(T_copied, NT * t + copied)
                    if not (isinstance(t, int) and NK * t + c < KB):
                        pe.wait_ge(key_used, NK * t + c - KB + 1)
                    pe.sem_inc(pe_passed, 1)
                    for s in range(KC):
                        one, seg = maskT[:, b, c * KC + s, :], key_banks[c % KB][:, s * P:(s + 1) * P]
                        pe.matmul(seg, one, down_b[:], start=True, stop=False)
                        last = pe.matmul(seg, one, seg_b[:, c * KC + s, :], start=False, stop=True)
                    last.then_inc(key_ready, 1)

            def turn_degree(q):
                pe.wait_ge(deg_ready, q + 1)
                if q:
                    pe.wait_ge(slots_known, q)
                pe.matmul(p_small[0:1, q * P:(q + 1) * P], degree[:, q:q + 1], ident[:], start=True, stop=True).then_inc(degT_ready, 1)

            def turn_ranked(g):
                pe.wait_ge(deg_ready, GR + g)
                if not (isinstance(g, int) and g < 2):
                    pe.wait_ge(grp_copied, 4 * (g - 2) + 3)
                    pe.sem_inc(pe_passed, 1)
                for r in range(GR):
                    last = pe.matmul(p_small[0:1, r * P:(r + 1) * P], ranked_degree[:, r:r + 1], ident[:], start=True, stop=True)
                last.then_inc(degT_ready, 1)

            def turn_h2(g):
                pe.wait_ge(h2_ready, g + 1)
                if not (isinstance(g, int) and g == 0):
                    pe.wait_ge(grp_copied, 4 * g)
                for q in range(GR):
                    last = pe.transpose(p_grp[:, q * P:(q + 1) * P], h2[:, q, :], ident[:])
                last.then_inc(grp_mm, 1)

            def make_WhT(g):
                pe.wait_ge(grp_copied, 4 * g + 1)
                pe.matmul(p_grp[:], W_sb[:], h2T_g[:], start=True, stop=True).then_inc(grp_mm, 1)

            def make_s_and_t(g, sorted_groups):
                pe.wait_ge(grp_copied, 4 * g + 2)
                pe.wait_ge(slots_known, GR + sorted_groups)
                for q in range(GR):
                    pe.matmul(p_small[:, P + q:P + q + 1], WhT_g[:, q * P:(q + 1) * P], a_sb[:, 1:2], start=True, stop=True)
                pe.matmul(p_grp[:], a1_all[:], WhT_g[:], start=True, stop=True).then_inc(grp_mm, 1)

            def make_Wh(g):
                pe.wait_ge(grp_copied, 4 * g + 3)
                for q in range(GR):
                    last = pe.matmul(p_grp[:, q * P:(q + 1) * P], h2T_g[:, q * P:(q + 1) * P], W_sb[:], start=True, stop=True)
                last.then_inc(grp_mm, 1)

            def multiply(g, q, d, n, banks, added):
                I, J = group_of(g, q, d)
                pe.wait_ge(att_added, added)
                for j in range(GR):
                    pe.wait_ge(w_ready, AHEAD + GR * n + j + 1)
                    for i in range(GR):
                        last = pe.matmul(banks[i // 2][:, i % 2 * D1:(i % 2 + 1) * D1], weights[:, j, i * P:(i + 1) * P],
                                         Whg[:, bass.ds(GR * J + j, 1), :].rearrange("p t d -> p (t d)"),
                                         start=(j == 0 and i % 2 == 0), stop=(j == GR - 1 and i % 2 == 1),
                                         skip_group_check=True)
                    last.then_inc(w_used, 1)

            def attend(g, q, k):
                if k == 0:
                    pe.wait_ge(grp_copied, 4 * g + 4)
                part(pe, g, q, k, k + 1, lambda d, n, k: multiply(g, q, d, n, p_att, n + 1))

            def attend_last(g, q):
                pe.wait_ge(grp_copied, 4 * g + 4)
                first, blocks, number, _ = lump(g, q)
                for k in range(blocks):
                    n = number + k
                    multiply(g, q, first + k, n, pair_of(n), n + 1 if n == FIRST_LAST else n)
                    if (g, q, k) == (NG - 3, 2, 0):
                        turn_h2(NG - 2)
                    elif (g, q, k) == (NG - 3, 2, 1):
                        make_WhT(NG - 2)
                    elif (g, q, k) == (NG - 3, 3, 0):
                        make_s_and_t(NG - 2, NG - 1)
                    elif (g, q, k) == (NG - 3, 3, 1):
                        make_Wh(NG - 2)
                    elif (g, q, k) == (NG - 2, 2, 2):
                        turn_h2(NG - 1)
                    elif (g, q, k) == (NG - 2, 3, 0):
                        make_WhT(NG - 1)
                    elif (g, q, k) == (NG - 2, 3, 1):
                        make_s_and_t(NG - 1, NG - 1)
                    elif (g, q, k) == (NG - 2, 3, 2):
                        make_Wh(NG - 1)

            pe.wait_ge(consts, 4)
            transposes(0)
            pe.wait_ge(consts, 7)
            for q in range(GR):
                keys(q, q % 2)
                if q == 1:
                    pe.wait_ge(w_in, 48)
                    pe.transpose(p_grp[:, 0:D], W_sb[:], ident[:]).then_inc(WT_ready, 1)
                    pe.wait_ge(WT_copied, 1)
                    pe.wait_ge(slots_known, 1)
                    pe.matmul(p_small[:, 0:2], WT_sb[:], a_sb[:], start=True, stop=True).then_inc(Wa_ready, 1)
                    pe.wait_ge(Wa_sq, 1)
                    pe.matmul(p_small[:, 0:2], ones[:], Wa[:], start=True, stop=True).then_inc(norm_ready, 1)
                    pe.wait_ge(bound_ready, 1)
                transposes(q + 1)
                turn_degree(q)

            def step(g, q):
                t = GR * (g + 1) + q
                now = due(g, q)

                done = not (isinstance(g, int) and g == 0)
                keys(t, q % 2)
                if q == 3 and done:
                    make_Wh(g - 1)
                if q == 2 and done:
                    turn_h2(g - 1)
                if now:
                    attend(*now, 0)
                if q == 2 and done:
                    make_WhT(g - 1)
                if q == GR - 1:
                    unless_last(pe, g, lambda: transposes(t + 1))
                if now:
                    attend(*now, 1)
                if q == GR - 1:
                    turn_ranked(g + 1)
                else:
                    transposes(t + 1)
                if q == 2 and done:
                    make_s_and_t(g - 1, g)
                if now:
                    attend(*now, 2)

            over_groups(pe, step)
            assert lump(NG - 3, 2)[1] >= 2 and lump(NG - 3, 3)[1] >= 2 and lump(NG - 2, 2)[1] >= 3 and lump(NG - 2, 3)[1] >= 3
            for q in range(1, GR):
                attend_last(NG - 3, q)
            for q in range(GR):
                attend_last(NG - 2, q)
            for q in range(GR):
                attend_last(NG - 1, q)
            pe.wait_ge(lost_ready, 1)
            pe.matmul(p_small[0:1, 0:1], lost_row[:, 0:1], ones[:, 0:1], start=True, stop=True).then_inc(lost_sum, 1)

            pe.wait_ge(redo_known, 1)
            with pe.If(pe.value_load(redo[0:1, 0:1], min_val=0, max_val=1)):
                pe.wait_ge(h2_all, 1)
                for g in range(T // 4):
                    if g >= 2:
                        pe.wait_ge(hT_copied, g - 1)
                    for q in range(4):
                        last = pe.transpose(p_key[g % 2][:, q * P:(q + 1) * P], h_sb[:, 4 * g + q, :], ident[:])
                    last.then_inc(hT_ready, 1)
                for g in range(T // 4):
                    pe.wait_ge(hT_copied, g + 1)
                    if g:
                        pe.wait_ge(W_copied, 4 * g)
                    else:
                        pe.wait_ge(hT_copied, T // 4)
                    pe.matmul(p_att[0][:], W_sb[:], h2T[:, g * 512:(g + 1) * 512], start=True, stop=True).then_inc(W_mm, 1)
                    for q in range(4):
                        last = pe.matmul(p_att[1][:, q * P:(q + 1) * P], h2T[:, (4 * g + q) * P:(4 * g + q + 1) * P], W_sb[:],
                                         start=True, stop=True)
                    last.then_inc(W_mm, 1)
                    pe.wait_ge(W_copied, 4 * g + 1)
                    pe.matmul(p_key[0][:], a2_all[:], WhT[:, g * 512:(g + 1) * 512], start=True, stop=True)
                    for q in range(4):
                        last = pe.matmul(p_small[:, 8 + q:9 + q], WhT[:, (4 * g + q) * P:(4 * g + q + 1) * P], a_sb[:, 0:1],
                                         start=True, stop=True)
                    last.then_inc(W_mm, 1)

                def attend_row(t, b, first):
                    pe.wait_ge(e_ready, t + 1)
                    for g in range(T // 4):
                        if first and g < 2:
                            pe.wait_ge(W_copied, T)
                        else:
                            pe.wait_ge(eT_copied, t * (T // 4) + g - 1)
                        for q in range(4):
                            last = pe.transpose(p_key[g % 2][:, q * P:(q + 1) * P], G0[:, 4 * g + q, :], ident[:])
                        last.then_inc(eT_ready, 1)
                    if not first:
                        pe.wait_ge(hm_ready, t - 1 if b else t)
                    for g in range(T // 4):
                        pe.wait_ge(eT_copied, t * (T // 4) + g + 1)
                        for q in range(4):
                            j = 4 * g + q
                            last = pe.matmul(p_att[b][:, 0:D], h_sb[:, j, :], Wh[:, j, :], start=(j == 0), stop=(j == T - 1))
                    last.then_inc(av_ready, 1)

                attend_row(0, 0, True)
                attend_row(1, 1, False)
                with pe.Fori(1, T // 2) as i:
                    for b in range(2):
                        attend_row(2 * i + b, b, False)

        @block.vector
        def _(dve):
            V = nc.vector

            def then(ins):
                dve.drain()
                return ins

            def wait(s, value):
                dve.wait_ge(s, value)
                dve.sem_inc(passed, 1)

            V.memset(landed_i[:], 0)
            V.memset(is_rank[:], 0.0)
            dve.drain()
            for q in range(GR):
                V.memset(place[:, q:q + 1], float(q))
                V.memset(is_rank[:, q, q:q + 1], 1.0)
            dve.drain()
            dve.sem_inc(w_used, GR)
            dve.sem_inc(w_ready, AHEAD)
            dve.sem_inc(att_added, 1)
            def moments(g):
                for q in range(GR):
                    V.bn_stats(stats[:, q, :], x_sb[:, bass.ds(GR * g + q, 1), :].rearrange("p t d -> p (t d)"))
                dve.drain()
                for q in range(GR):
                    V.bn_aggr(mv[:, q, :], stats[:, q, :])

            def variance(tiles):
                dve.drain()
                return V.tensor_scalar(rstd[:, tiles], mv[:, tiles, 1:2].rearrange("p t o -> p (t o)"), EPS, None, ALU.add)

            def scale_and_shift(tiles):
                then(V.reciprocal(rstd[:, tiles], rstd[:, tiles]))
                return V.scalar_tensor_tensor(shift[:, tiles], mv[:, tiles, 0:1].rearrange("p t o -> p (t o)"), -1.0,
                                              rstd[:, tiles], ALU.mult, ALU.mult)

            for c in range(XC):
                dve.wait_ge(x_in[c], 16)
                for t in range(XT):
                    V.bn_stats(stats[:, t, :], x_sb[:, c * XT + t, :])
                dve.drain()
                for t in range(XT):
                    V.bn_aggr(mv[:, c * XT + t, :], stats[:, t, :])
                dve.drain()
            variance(slice(0, T)).then_inc(var_ready, 1)

            def find(t, b):
                for c in range(NK):
                    wait(key_ready, NK * t + c + 1)
                    for s in range(KC):
                        j = c * KC + s
                        last = V.max(cand[:, j * TOP:(j + 1) * TOP], key_banks[c % KB][:, s * P:(s + 1) * P])
                    last.then_inc(key_used, 1)

            def take(q, r):
                then(V.max(nbrs[:, q, r * TOP:(r + 1) * TOP], cand[:]))

            def drop(q, r):
                then(V.match_replace(cand[:], nbrs[:, q, r * TOP:(r + 1) * TOP], cand[:], 0.0))

            def begin_lists(t, q):
                dve.drain()
                V.tensor_reduce(lost[:, 0, bass.ds(t, 1)], cand[:].rearrange("p (s k) -> p s k", k=TOP)[:, :, TOP - 1], axis=X, op=ALU.max)
                for r in range(2):
                    take(q, r)
                    drop(q, r)

            def end_lists(t, q):
                for r in range(2, SLOTS // TOP):
                    if r > 2:
                        drop(q, r - 1)
                    take(q, r)
                then(V.tensor_scalar(junk[:], nbrs[:, q], 0.0, None, ALU.is_gt, ALU.add, accum_out=degree[:, q:q + 1]))
                V.scalar_tensor_tensor(lost[:, 1, bass.ds(t, 1)], sign_sum[:, q % 2:q % 2 + 1], degree[:, q:q + 1],
                                       nbrs[:, q, SLOTS - 1:SLOTS], ALU.not_equal, ALU.max).then_inc(listed, 1)

            def rank_lists():
                then(V.scalar_tensor_tensor(tie_broken[:], degree[:], float(GR), place[:], ALU.mult, ALU.add))
                for t in range(GR):
                    V.tensor_scalar(of_rank[:, t, :], tie_broken[:], tie_broken[:, t:t + 1], None, ALU.is_gt, ALU.add,
                                    accum_out=rank[:, t:t + 1])
                dve.drain()
                for t in range(GR):
                    V.tensor_scalar(is_rank_next[:, t, :], place[:], rank[:, t:t + 1], None, ALU.is_equal)
                dve.drain()
                then(V.tensor_tensor(of_rank[:], is_rank_next[:], degree[:].unsqueeze(2).to_broadcast([P, GR, GR]), ALU.mult))
                V.tensor_reduce(ranked_degree[:], of_rank[:].rearrange("p t r -> p r t"), axis=X, op=ALU.add).then_inc(deg_ready, 1)
                for t in range(GR):
                    for r in range(GR):
                        if t == 0:
                            V.tensor_scalar(ranked[:, r], nbrs[:, t], is_rank_next[:, t, r:r + 1], None, ALU.mult)
                        else:
                            V.scalar_tensor_tensor(ranked[:, r], nbrs[:, t], is_rank_next[:, t, r:r + 1], ranked[:, r], ALU.mult, ALU.add)
                    dve.drain()

            def count(first, n, done):
                dve.wait_ge(degT_ready, done)
                V.tensor_reduce(deg_max[:, first:first + n], p_small[0:1, first * P:(first + n) * P].rearrange("p (r c) -> p r c", r=n),
                                axis=X, op=ALU.max).then_inc(slots_known, 1)
                dve.drain()
                then(V.tensor_scalar(deg_max[:, first:first + n], deg_max[:, first:first + n], float(SURE), None, ALU.max))

            def publish(lists, first, n):
                those = slice(first, first + n)
                V.tensor_copy(n_slots[:, those], deg_max[:, those])
                V.tensor_scalar(idx[:, those], lists[:, those], -1.0, float(N), ALU.mult, ALU.add)
                for q in range(first, first + n):
                    two_back = (q + 2) % GR
                    then(V.scalar_tensor_tensor(landed_i[:, q:q + 1], deg_max[:, q:q + 1], 16.0,
                                                landed_i[:, two_back:two_back + 1], ALU.mult, ALU.add))
                dve.sem_inc(lists_ready, n)

            def reduce(q):
                b, often = q % 2, OFTEN[q]
                landed = dve.value_load(landed_i[0:1, q:q + 1], min_val=16, max_val=16 * SLOTS * T)
                n = dve.value_load(n_slots[0:1, q:q + 1], min_val=SURE, max_val=SLOTS)
                dve.wait_ge(gathered[b], landed)
                V.tensor_reduce(nbr_rows[:, q], G[:, b, 0:often].rearrange("p k d -> p d k"), axis=X, op=ALU.max)
                with dve.If(n > often):
                    then(V.tensor_reduce(more_row[:], G[:, b, often:].rearrange("p k d -> p d k"), axis=X, op=ALU.max))
                    V.tensor_tensor(nbr_rows[:, q], nbr_rows[:, q], more_row[:], ALU.max)
                dve.drain()
                dve.sem_inc(reduced, 1)

            def restore(g):
                for r in range(GR):
                    for t in range(GR):
                        tile = x_sb[:, bass.ds(GR * g + t, 1), :].rearrange("p t d -> p (t d)")
                        V.scalar_tensor_tensor(tile, nbr_rows[:, r], is_rank[:, t, r:r + 1], tile, ALU.mult, ALU.add)
                    dve.drain()
                moments(g)
                if not (isinstance(g, int) and g == NG - 1):
                    V.tensor_copy(is_rank[:], is_rank_next[:])
                variance(slice(0, GR)).then_inc(var_ready, 1)

            def attend_in(g, q):
                wait(grp_copied, 4 * g + 4)
                wait(M_in[q % 2], 16 * lump(g, q)[3])

            def weigh(g, q, d, n, k):
                I, J = group_of(g, q, d)
                r = r_all[:, bass.ds(GP * I, GP)].rearrange("p (i r) -> p i r", i=GR)
                for j in range(GR):
                    dve.wait_ge(w_used, GR * n + j + 1)
                    mask = (M[:, q % 2, k, :, j * P:(j + 1) * P] if isinstance(k, int) else
                            M[:, q % 2, bass.ds(k, 1), :, j * P:(j + 1) * P].rearrange("p n i q -> p (n i) q"))
                    V.scalar_tensor_tensor(weights[:, j, :].rearrange("p (i r) -> p i r", i=GR), r,
                                           lam[:, bass.ds(GR * J + j, 1)], mask, ALU.max, ALU.mult).then_inc(w_ready, 1)

            def add_up(g, q, d, n, banks=p_att):
                I, J = group_of(g, q, d)
                dve.wait_ge(w_used, GR * n + 2 * GR)
                for h in range(2):
                    rows_h = attended[:, bass.ds(GR * I + 2 * h, 2), :].rearrange("p t d -> p (t d)")
                    last = V.tensor_tensor(rows_h, rows_h, banks[h][:, 0:2 * D1], ALU.add)
                last.then_inc(att_added, 1)

            def weigh_one(now, k):
                if now:
                    part(dve, *now, k, k + 1, lambda d, n, k: weigh(*now, d, n, k))

            def add_one(now, k):
                if now:
                    part(dve, *now, k, k + 1, lambda d, n, k: add_up(*now, d, n))

            dve.wait_ge(std_ready, 1)
            scale_and_shift(slice(0, T)).then_inc(shift_ready, 1)
            find(0, 0)
            begin_lists(0, 0)
            end_lists(0, 0)
            dve.sem_inc(deg_ready, 1)
            count(0, 1, 1)
            publish(nbrs, 0, 1)
            dve.wait_ge(w_in, 48)
            dve.wait_ge(consts, 1)
            V.tensor_scalar(a1_all[:], ones[:], a_sb[:, 0:1], None, ALU.mult)
            V.tensor_scalar(a2_all[:], ones[:], a_sb[:, 1:2], None, ALU.mult)
            for q in range(1, GR):
                find(q, q % 2)
                begin_lists(q, q)
                end_lists(q, q)
                dve.sem_inc(deg_ready, 1)
                if q == 1:
                    dve.wait_ge(Wa_ready, 1)
                    then(V.tensor_copy(bound[:], p_small[:, 0:2]))
                    V.tensor_tensor(Wa[:], bound[:], bound[:], ALU.mult).then_inc(Wa_sq, 1)
                    dve.wait_ge(bound_ready, 1)
                    then(V.tensor_scalar(g_bias[:], bound[:, 1:2], -SLACK, None, ALU.mult))
                    then(V.tensor_tensor(r_bias[:], bound[:, 0:1], bound[:, 1:2], ALU.max))
                    V.tensor_scalar(r_bias[:], r_bias[:], -REST * SLACK, None, ALU.mult).then_inc(bias_ready, 1)
                count(q, 1, q + 1)
                publish(nbrs, q, 1)
            dve.wait_ge(h_ready, XC)
            reduce(0)
            dve.wait_ge(consts, 9)

            def step(g, q):
                t = GR * (g + 1) + q
                now = due(g, q)
                if now and isinstance(now[0], int) and lump(*now)[1] == 0:
                    now = None
                done = not (isinstance(g, int) and g == 0)
                if now and q < GR - 1:
                    attend_in(*now)
                    weigh_one(now, 0)
                find(t, q % 2)
                if q == 1 and done:
                    wait(std_ready, g + 1)
                    scale_and_shift(slice(0, GR)).then_inc(shift_ready, 1)
                if now and q == GR - 1:
                    attend_in(*now)
                    weigh_one(now, 0)
                begin_lists(t, q)
                add_one(now, 0)
                weigh_one(now, 1)
                end_lists(t, q)
                if q == GR - 1:
                    dve.drain()
                    rank_lists()
                add_one(now, 1)
                weigh_one(now, 2)
                if done and q:
                    reduce(q - 1)
                elif done:
                    reduce(GR - 1)
                    publish(ranked, GR - 1, 1)
                elif q % 2:
                    reduce((q + 1) // 2)
                if q == GR - 1:
                    count(0, GR, GR + g + 1)
                    publish(ranked, 0, GR - 1)
                add_one(now, 2)
                if q == 0 and done:
                    restore(g - 1)

            over_groups(dve, step)

            def attend_last(g, q, ks=None, before=None, after=None):
                attend_in(g, q)
                first, blocks, number, _ = lump(g, q)
                for k in ks or range(blocks):
                    weigh(g, q, first + k, number + k, k)
                    if before:
                        add_last(before, after)
                    before = (g, q, first + k, number + k)
                return before

            def add_last(block, after=None):
                g, q, d, n = block
                add_up(g, q, d, n, pair_of(n))
                dve.drain()
                if after and g == NG - 1 and q < 2:
                    after(d)

            EARLY = 2
            block = attend_last(NG - 3, 1)
            reduce(GR - 1)
            publish(ranked, GR - 1, 1)
            add_last(block)
            restore(NG - 2)
            block = attend_last(NG - 3, 2)
            dve.wait_ge(std_ready, NG)
            scale_and_shift(slice(0, GR)).then_inc(shift_ready, 1)
            block = attend_last(NG - 3, 3, before=block)
            reduce(0)
            add_last(block)
            block = attend_last(NG - 2, 0)
            reduce(1)
            add_last(block)
            block = attend_last(NG - 2, 1, range(EARLY))
            reduce(2)
            add_last(block)
            block = attend_last(NG - 2, 1, range(EARLY, lump(NG - 2, 1)[1]))
            block = attend_last(NG - 2, 2, range(EARLY), block)
            reduce(GR - 1)
            add_last(block)
            restore(NG - 1)
            block = attend_last(NG - 2, 2, range(EARLY, lump(NG - 2, 2)[1]))
            dve.wait_ge(std_ready, NG + 1)
            scale_and_shift(slice(0, GR)).then_inc(shift_ready, 1)
            block = attend_last(NG - 2, 3, before=block)

            def divide(I):
                tiles = slice(GR * I, GR * (I + 1))
                then(V.tensor_scalar(rden[:, tiles], attended[:, tiles, D:D1].rearrange("p t o -> p (t o)"), LEAST_DEN, None, ALU.max))
                then(V.reciprocal(rden[:, tiles], rden[:, tiles]))
                V.tensor_scalar(neg_rden[:, tiles], rden[:, tiles], -1.0, None, ALU.mult).then_inc(divisor_ready, 1)

            def after(I):
                if I < NG - 1:
                    divide(I)
            for q in range(GR):
                block = attend_last(NG - 1, q, before=block, after=after)
            add_last(block)
            divide(NG - 1)
            dens = attended[:, :, D:D1].rearrange("p t o -> p (t o)")
            V.tensor_scalar(g_col[:], dens, LEAST_DEN, None, ALU.is_ge)
            V.tensor_scalar(lam[:], dens, MOST_DEN, None, ALU.is_le)
            dve.drain()
            then(V.tensor_tensor(g_col[:], g_col[:], lam[:], ALU.mult))
            then(V.tensor_reduce(lost_row[:, 1:2], g_col[:], axis=X, op=ALU.add))
            then(V.tensor_reduce(lost_row[:, 0:1], lost[:].rearrange("p k t -> p (k t)"), axis=X, op=ALU.max))
            then(V.tensor_scalar(lost_row[:, 1:2], lost_row[:, 1:2], float(T), None, ALU.not_equal))
            V.tensor_tensor(lost_row[:, 0:1], lost_row[:, 0:1], lost_row[:, 1:2], ALU.add).then_inc(lost_ready, 1)
            dve.wait_ge(lost_sum, 1)
            V.tensor_scalar(redo[:], p_small[0:1, 0:1], 0.5, None, ALU.is_gt).then_inc(redo_known, 1)
            dve.wait_ge(redo_known, 1)

            with dve.If(dve.value_load(redo[0:1, 0:1], min_val=0, max_val=1)):
                dve.sem_inc(back_tile, 1)
                dve.sem_inc(back_used, 2)
                with dve.Fori(0, T) as t:
                    acc = nbr_max[:, bass.ds(t, 1), :].rearrange("p t d -> p (t d)")
                    dve.wait_ge(back_adj, 16 * (t + 1))
                    V.tensor_scalar(key, adj_t[:, 0], 0, None, ALU.not_equal).then_inc(back_tile, 1)
                    V.tensor_scalar(acc, ones[:], 0.0, None, ALU.mult)
                    dve.drain()
                    with dve.Fori(0, CH // 2) as c:
                        for b in range(2):
                            dve.wait_ge(back_h[b], t * (16 * CH // 2) + 16 * c + 16)
                            for r in range(T):
                                j = (2 * c + b) * T + r
                                then(V.scalar_tensor_tensor(acc, G[:, b, r, :], key[:, bass.ds(j, 1)], acc, ALU.mult, ALU.max))
                            dve.sem_inc(back_used, 1)
                dve.wait_ge(x_again, 16 * XC)
                then(V.tensor_tensor(x_sb[:], x_sb[:], nbr_max, ALU.add))
                for c in range(XC):
                    for t in range(XT):
                        V.bn_stats(stats[:, t, :], x_sb[:, c * XT + t, :])
                    dve.drain()
                    for t in range(XT):
                        V.bn_aggr(mv[:, c * XT + t, :], stats[:, t, :])
                    dve.drain()
                variance(slice(0, T)).then_inc(var2_ready, 1)
                dve.wait_ge(std2_ready, 1)
                then(scale_and_shift(slice(0, T)))
                with dve.Fori(0, T) as t:
                    V.tensor_scalar(h_sb[:, bass.ds(t, 1), :], x_sb[:, bass.ds(t, 1), :], rstd[:, bass.ds(t, 1)],
                                    shift[:, bass.ds(t, 1)], ALU.mult, ALU.add)
                dve.drain()
                V.tensor_scalar(h_sb, h_sb, 0.0, None, ALU.max).then_inc(h2_all, 1)
                dve.wait_ge(W_copied, T)

                def attend_row(i, b, first):
                    t = 2 * i + b
                    dve.wait_ge(adj2_in[b], 16 * (i + 1))
                    if not first:
                        dve.wait_ge(eT_ready, t * (T // 4))
                    Z = G0.rearrange("p k d -> p (k d)")
                    F = G1.rearrange("p k d -> p (k d)")
                    then(V.tensor_scalar(Z, r_all[:], s_col[:, bass.ds(t, 1)], None, ALU.add))
                    then(V.scalar_tensor_tensor(Z, Z, ALPHA, Z, ALU.mult, ALU.max))
                    then(V.tensor_scalar(F, adj_t[:, b], 0, -2.0 * NEG_FILL, ALU.is_gt, ALU.mult).then_inc(adj2_used, 1))
                    then(V.scalar_tensor_tensor(Z, F, NEG_FILL, Z, ALU.add, ALU.min))
                    V.tensor_reduce(neg_max[:, b:b + 1], Z, axis=X, op=ALU.max, negate=True).then_inc(z_ready, 1)
                    dve.wait_ge(av_ready, t + 1)
                    then(V.reciprocal(rden[:, b:b + 1], den[:, b:b + 1]))
                    then(V.tensor_scalar(hp[:], p_att[b][:, 0:D], rden[:, b:b + 1], None, ALU.mult))
                    V.tensor_scalar(hm[:], hp[:], 0.0, None, ALU.min).then_inc(hm_ready, 1)
                    if not first:
                        dve.wait_ge(stored[b], 16 * i)
                    then(V.scalar_tensor_tensor(hp[:], hp[:], 0.0, x_sb[:, bass.ds(t, 1), :].rearrange("p t d -> p (t d)"), ALU.max, ALU.add))
                    dve.wait_ge(he_ready, t + 1)
                    V.scalar_tensor_tensor(res[:, b], he[:], -1.0, hp[:], ALU.add, ALU.add).then_inc(res_ready, 1)

                attend_row(0, 0, True)
                dve.wait_ge(eT_ready, T // 4)
                attend_row(0, 1, True)
                with dve.Fori(1, T // 2) as i:
                    for b in range(2):
                        attend_row(i, b, False)


_INS = ["x", "adj", "L1_gnn_W", "L1_gnn_a"]


def kernel(**inputs):
    import numpy as np
    import concourse.bacc as bacc
    from concourse import mybir as mb
    from concourse.bass_utils import run_bass_kernel_spmd as run

    nc = bacc.Bacc("TRN2", target_bir_lowering=False, num_devices=1)
    arrays, args = {}, []
    for name in _INS:
        arr = np.ascontiguousarray(inputs[name])
        arrays[f"in_{name}"] = arr
        args.append(nc.dram_tensor(f"in_{name}", arr.shape, mb.dt.from_np(arr.dtype), kind="ExternalInput").ap())
    shape = inputs["x"].shape
    out = nc.dram_tensor("out", shape, mb.dt.float32, kind="ExternalOutput").ap()
    gnn_layers(nc, *args, out)
    r = run(nc, [arrays], core_ids=[0])
    return r.results[0]["out"]
```
